# Optimizing a Trainium2 kernel written in Bass

```python
import numpy as np
import jax
import jax.numpy as jnp

def _softmax(x, axis=-1):
    return jax.nn.softmax(x, axis=axis)

def _gelu(x):
    return jax.nn.gelu(x, approximate=True)

def _silu(x):
    return jax.nn.silu(x)

def _sigmoid(x):
    return jax.nn.sigmoid(x)

def _layernorm(x, axis=-1, eps=1e-05):
    m = jnp.mean(x, axis=axis, keepdims=True)
    v = jnp.var(x, axis=axis, keepdims=True)
    return (x - m) / jnp.sqrt(v + eps)

def _scatter_add(tgt, idx, src, axis=0):
    return tgt.at[idx].add(src)

def _segment_sum(src, seg, n):
    return jax.ops.segment_sum(src, seg, n)
kernel_name = 'mk_flamingo_gated_d1_seqx_r8_93fcab'

def setup_inputs(seed: int=0):
    np.random.seed(seed)
    _w = jnp.asarray

    def _rec_inputs():
        import jax
        import jax.numpy as jnp
        _rk = jax.random.key(seed)
        x = -0.0003929 + 0.9999 * jax.random.normal(jax.random.fold_in(_rk, 1), (8, 56, 512), jnp.float32)
        _lenS = 56 - jax.random.randint(jax.random.fold_in(_rk, 7), (8,), 0, max(1, 56 // 4) + 1, jnp.int32)
        _lenS2 = 1500 - jax.random.randint(jax.random.fold_in(_rk, 8), (8,), 0, max(1, 1500 // 4) + 1, jnp.int32)
        _ctx_4096P = jax.random.normal(jax.random.fold_in(_rk, 11), (8, 16, 512), jnp.float32)
        _ctx_4096c = jax.random.dirichlet(jax.random.fold_in(_rk, 511), 0.3 * jnp.ones((16,), jnp.float32), (8, 1500))
        _ctx_4096t = jnp.einsum('bsk,bkd->bsd', _ctx_4096c, _ctx_4096P)
        _ctx_4096t = _ctx_4096t * jax.lax.rsqrt(jnp.mean(jnp.square(_ctx_4096t)) + 1e-12) * 0.953939
        ctx_4096 = 2.81802e-05 + 1.00001 * (_ctx_4096t + 0.3 * jax.random.normal(jax.random.fold_in(_rk, 611), (8, 1500, 512), jnp.float32))
        _g = jax.random.normal(jax.random.fold_in(_rk, 9001), (2, 1), jnp.float32)
        _g = jnp.sign(_g) * jnp.maximum(jnp.abs(_g), 1.0) + (_g == 0) * 1.0
        g_xattn = _g[0]
        g_ffn = _g[1]
        return (x, ctx_4096, g_xattn, g_ffn)
    x, ctx_4096, g_xattn, g_ffn = _rec_inputs()

    def _L0_xattn_setup():
        import jax, jax.numpy as jnp
        import numpy as np
        B, S, F = (2, 256, 512)
        HQ, HKV, D = (32, 8, 128)
        REP = HQ // HKV
        key = jax.random.key(seed)
        ks = jax.random.split(key, 6)
        scale = 0.02
        return {'query': jax.random.normal(ks[0], (B, S, F), jnp.float32), 'value': jax.random.normal(ks[1], (B, S, F), jnp.float32), 'wq': jax.random.normal(ks[2], (F, HQ * D), jnp.float32) * scale, 'wk': jax.random.normal(ks[3], (F, HKV * D), jnp.float32) * scale, 'wv': jax.random.normal(ks[4], (F, HKV * D), jnp.float32) * scale, 'wo': jax.random.normal(ks[5], (HQ * D, F), jnp.float32) * scale}
    _L0_xattn_all = _L0_xattn_setup()
    _L0_xattn_in = {k: v for k, v in _L0_xattn_all.items() if k in ('wq', 'wk', 'wv', 'wo')}
    del _L0_xattn_all

    def _L0_ffn_setup():
        import jax, jax.numpy as jnp
        import numpy as np
        LORA_SCALING = 1.0 / 2.0

        def _qlora_linear(x, wq, A, B):
            w = jnp.tile(wq, (1, 4))
            base = x @ w.T
            lora = x @ A.T @ B.T
            return base + lora * LORA_SCALING
        key = jax.random.key(seed)
        ks = jax.random.split(key, 10)
        d, h, r = (512, 1376, 2)
        return {'x': jax.random.normal(ks[0], (16, 1, d), dtype=jnp.float32), 'w1q': jax.random.normal(ks[1], (h, d // 4), dtype=jnp.float32) * 0.02, 'a1': jax.random.normal(ks[2], (r, d), dtype=jnp.float32) * 0.02, 'b1': jax.random.normal(ks[3], (h, r), dtype=jnp.float32) * 0.02, 'w3q': jax.random.normal(ks[4], (h, d // 4), dtype=jnp.float32) * 0.02, 'a3': jax.random.normal(ks[5], (r, d), dtype=jnp.float32) * 0.02, 'b3': jax.random.normal(ks[6], (h, r), dtype=jnp.float32) * 0.02, 'w2q': jax.random.normal(ks[7], (d, h // 4), dtype=jnp.float32) * 0.02, 'a2': jax.random.normal(ks[8], (r, h), dtype=jnp.float32) * 0.02, 'b2': jax.random.normal(ks[9], (d, r), dtype=jnp.float32) * 0.02}
    _L0_ffn_all = _L0_ffn_setup()
    _L0_ffn_in = {k: v for k, v in _L0_ffn_all.items() if k in ('w1q', 'a1', 'b1', 'w3q', 'a3', 'b3', 'w2q', 'a2', 'b2')}
    del _L0_ffn_all
    return {'x': x, 'ctx_4096': ctx_4096, 'g_xattn': g_xattn, 'g_ffn': g_ffn, 'L0_xattn_wq': _L0_xattn_in['wq'], 'L0_xattn_wk': _L0_xattn_in['wk'], 'L0_xattn_wv': _L0_xattn_in['wv'], 'L0_xattn_wo': _L0_xattn_in['wo'], 'L0_ffn_w1q': _L0_ffn_in['w1q'], 'L0_ffn_a1': _L0_ffn_in['a1'], 'L0_ffn_b1': _L0_ffn_in['b1'], 'L0_ffn_w3q': _L0_ffn_in['w3q'], 'L0_ffn_a3': _L0_ffn_in['a3'], 'L0_ffn_b3': _L0_ffn_in['b3'], 'L0_ffn_w2q': _L0_ffn_in['w2q'], 'L0_ffn_a2': _L0_ffn_in['a2'], 'L0_ffn_b2': _L0_ffn_in['b2']}

def reference(x, ctx_4096, g_xattn, g_ffn, L0_xattn_wq, L0_xattn_wk, L0_xattn_wv, L0_xattn_wo, L0_ffn_w1q, L0_ffn_a1, L0_ffn_b1, L0_ffn_w3q, L0_ffn_a3, L0_ffn_b3, L0_ffn_w2q, L0_ffn_a2, L0_ffn_b2):
    import jax
    import jax.numpy as jnp

    def _L0_xattn_ref(query, value, wq, wk, wv, wo):
        import jax, jax.numpy as jnp
        import numpy as np
        B, S, F = (2, 256, 512)
        HQ, HKV, D = (32, 8, 128)
        REP = HQ // HKV
        key = value
        b, tq, _ = query.shape
        tk = key.shape[1]
        q = (query @ wq).reshape(b, tq, HQ, D)
        k = (key @ wk).reshape(b, tk, HKV, D)
        v = (value @ wv).reshape(b, tk, HKV, D)
        k = jnp.repeat(k, REP, axis=2)
        v = jnp.repeat(v, REP, axis=2)
        q = q * (1.0 / jnp.sqrt(jnp.asarray(D, q.dtype)))
        scores = jnp.einsum('bqhd,bkhd->bhqk', q, k)
        probs = jax.nn.softmax(scores, axis=-1)
        out = jnp.einsum('bhqk,bkhd->bqhd', probs, v).reshape(b, tq, HQ * D)
        return out @ wo

    def _L0_ffn_ref(x, w1q, a1, b1, w3q, a3, b3, w2q, a2, b2):
        import jax, jax.numpy as jnp
        import numpy as np
        LORA_SCALING = 1.0 / 2.0

        def _qlora_linear(x, wq, A, B):
            w = jnp.tile(wq, (1, 4))
            base = x @ w.T
            lora = x @ A.T @ B.T
            return base + lora * LORA_SCALING
        gate = jax.nn.silu(_qlora_linear(x, w1q, a1, b1))
        up = _qlora_linear(x, w3q, a3, b3)
        return _qlora_linear(gate * up, w2q, a2, b2)
    x = x + jnp.tanh(g_xattn[0]) * _L0_xattn_ref(_layernorm(x, axis=-1), ctx_4096, L0_xattn_wq, L0_xattn_wk, L0_xattn_wv, L0_xattn_wo)
    x = x + jnp.tanh(g_ffn[0]) * _L0_ffn_ref(_layernorm(x, axis=-1), L0_ffn_w1q, L0_ffn_a1, L0_ffn_b1, L0_ffn_w3q, L0_ffn_a3, L0_ffn_b3, L0_ffn_w2q, L0_ffn_a2, L0_ffn_b2)
    return x

_drawn_inputs = setup_inputs


def setup_inputs(seed=0):
    import zlib

    import numpy as np

    out = dict(_drawn_inputs(seed))
    spreads = {}
    factors = {'L0_xattn_wq': 3.655,
     'L0_xattn_wk': 3.659,
     'L0_ffn_a1': 8.0,
     'L0_ffn_b1': 8.0,
     'L0_ffn_a3': 8.0,
     'L0_ffn_b3': 8.0,
     'L0_ffn_a2': 8.0,
     'L0_ffn_b2': 8.0}
    for name, (base, spread) in spreads.items():
        noise = np.random.default_rng([zlib.crc32(name.encode()), seed]).standard_normal(out[name].shape)
        drawn = base * np.exp(spread * noise) if base else spread * noise
        out[name] = jnp.asarray(drawn.astype(out[name].dtype))
    for name, factor in factors.items():
        out[name] = (out[name] * factor).astype(out[name].dtype)
    return out
```

```python
from contextlib import ExitStack

import concourse.bass as bass
from concourse import mybir

F32 = mybir.dt.float32
F32R = mybir.dt.float32r
ALU = mybir.AluOpType
ACT = mybir.ActivationFunctionType
AX = mybir.AxisListType

B, TQ, F = 8, 56, 512
TK = 1500
HQ, HKV, D = 32, 8, 128
REP = HQ // HKV
HID = 1376
EPS = 1e-5
SCALE = 1.0 / float(D) ** 0.5
LORA = 0.5

NF = F // 128
TOK = B * TQ
TT = 112
NT = TOK // TT
G = 2
PAIRS = HKV // G
GH = HQ // G
QUARTERS = 4
CH = 125
NCH = TK // CH
PCH = (2, 4, 2, 4)
PC0 = tuple(sum(PCH[:q]) for q in range(QUARTERS))
PW = tuple(n * CH for n in PCH)
P0 = tuple(n * CH for n in PC0)
THIRDS = 3
T3 = TK // THIRDS
ROWS = 2 * TQ
CPB = 4
NPT = NCH // CPB
VW = 2 * D
HEADS4 = 4
NG4 = HQ // HEADS4
W4 = NF * HEADS4 * D

HQR = HID // 4
HCUT = [(0, 128), (128, 128), (256, HQR - 256)]
HCH = [(q * HQR + o, n, j) for q in range(4) for j, (o, n) in enumerate(HCUT)]

LN_USES = NF
Q_USES = HQ
V_USES = NCH
BODY = 2 * V_USES + PAIRS * (QUARTERS + 1)
GROUP = QUARTERS + B * BODY - QUARTERS
MAIN0 = LN_USES + Q_USES
END = MAIN0 + G * GROUP
U_V01 = 0
U_K = {1: V_USES, 2: V_USES + 5}
U_O = {0: V_USES + 4, 1: V_USES + 9, 2: V_USES + 10 + 16, 3: V_USES + 10 + 17 + 4}
U_KV = V_USES + 10
U_K0 = V_USES + 10 + 17
LOADS_G = 2 + B * QUARTERS
L_MAIN = NG4
L_WO = L_MAIN + G * LOADS_G
L_FFN = L_WO + NG4


def flamingo_kernel(nc, x, ctx, gx, gf, wq, wk, wv, wo, w1, w3, w2, a13, a2, b13, b2, out, q_dram, o_dram):
    es = ExitStack()
    with es:
        def sb(name, shape, dt=F32):
            return es.enter_context(nc.sbuf_tensor(name, shape, dt))

        def sem(name):
            return es.enter_context(nc.semaphore(name))

        stage = sb("stage", [128, 2, W4])
        wk_hi = sb("wk_hi", [128, W4], F32R)
        wk_lo = sb("wk_lo", [128, W4], F32R)
        wv_hi = sb("wv_hi", [128, W4], F32R)
        wv_lo = sb("wv_lo", [128, W4], F32R)
        cx_hi = sb("cx_hi", [128, NF * TK], F32R)
        cx_lo = sb("cx_lo", [128, NF * TK], F32R)
        v_hi = sb("v_hi", [128, NCH * VW], F32R)
        v_lo = sb("v_lo", [128, NCH * VW], F32R)
        k_hi = sb("k_hi", [128, TK], F32R)
        k_lo = sb("k_lo", [128, TK], F32R)
        qo = sb("qo", [128, GH * TOK])
        qs_hi = sb("qs_hi", [128, GH * TQ], F32R)
        qs_lo = sb("qs_lo", [128, GH * TQ], F32R)
        p_sb = sb("p_sb", [128, 2 * TK])
        pt = sb("pt", [128, NPT * CPB * 4 * ROWS], F32R)
        otmp = sb("otmp", [128, 2 * ROWS])
        ident = sb("ident", [128, 128])
        negmax = sb("negmax", [128, 2])
        psum_row = sb("psum_row", [128, 2])
        rinv = sb("rinv", [128, 2])
        stats = sb("stats", [128, NT, 6])
        mv = sb("mv", [128, NT, 2])
        std = sb("std", [128, NT])
        rstd = sb("rstd", [128, NT])
        gates = sb("gates", [128, 2])
        tgate = sb("tgate", [128, 2])
        a13_raw = sb("a13_raw", [128, NF, 4])
        a13_hi = sb("a13_hi", [128, NF, 4], F32R)
        a13_lo = sb("a13_lo", [128, NF, 4], F32R)
        a2_sb = sb("a2_sb", [128, len(HCH), 2])

        banks = es.enter_context(nc.psum_tensor("banks", [128, 8, 512], F32))
        ring = [banks[:, 6, :], banks[:, 7, :]]

        def w4(t):
            return t[:, :].rearrange("p (f n) -> p f n", f=NF)
        wkh, wkl, wvh, wvl = w4(wk_hi), w4(wk_lo), w4(wv_hi), w4(wv_lo)

        def part(t, q):
            return t[:, NF * P0[q]:NF * (P0[q] + PW[q])]

        cxh = [part(cx_hi, q).rearrange("p (f t) -> p f t", f=NF) for q in range(QUARTERS)]
        cxl = [part(cx_lo, q).rearrange("p (f t) -> p f t", f=NF) for q in range(QUARTERS)]
        vh = v_hi[:, :].rearrange("p (c n) -> p c n", c=NCH)
        vl = v_lo[:, :].rearrange("p (c n) -> p c n", c=NCH)
        qo3 = qo[:, :].rearrange("p (h t) -> p h t", h=GH)
        qsh3 = qs_hi[:, :].rearrange("p (h t) -> p h t", h=GH)
        qsl3 = qs_lo[:, :].rearrange("p (h t) -> p h t", h=GH)
        ph = p_sb[:, :].rearrange("p (h t) -> p h t", h=2)
        pt6 = pt[:, :].rearrange("p (g c s h r) -> p g c s h r", g=NPT, c=CPB, s=2, h=2)
        pt3 = pt[:, :].rearrange("p (c n) -> p c n", c=NCH)
        blk_hi = [cx_hi[:, s * W4:(s + 1) * W4].rearrange("p (f n) -> p f n", f=NF) for s in range(2)]
        blk_lo = [cx_lo[:, s * W4:(s + 1) * W4].rearrange("p (f n) -> p f n", f=NF) for s in range(2)]
        x_t = p_sb[0:TT, 0:NT * F].rearrange("p (t n) -> p t n", t=NT)
        XNW = F + 128
        xn_t = qo[0:TT, 0:NT * XNW].rearrange("p (t n) -> p t n", t=NT)
        xT = pt[:, 0:10 * TOK].rearrange("p (s f t) -> p s f t", s=2, f=NF + 1)
        ot_hi = [wk_hi[:, 0:HEADS4 * TOK], wv_hi[:, 0:HEADS4 * TOK]]
        ot_lo = [wk_lo[:, 0:HEADS4 * TOK], wv_lo[:, 0:HEADS4 * TOK]]
        w1h, w1l = cx_hi[:, 2 * W4:2 * W4 + HID], cx_lo[:, 2 * W4:2 * W4 + HID]
        w3h, w3l = v_hi[:, 0:HID], v_lo[:, 0:HID]
        w2h = v_hi[:, HID:HID + 3 * F].rearrange("p (j n) -> p j n", j=3)
        w2l = v_lo[:, HID:HID + 3 * F].rearrange("p (j n) -> p j n", j=3)
        o0 = NT * XNW
        b13_sb = qo[0:4, o0:o0 + 2 * HID].rearrange("p (s n) -> p s n", s=2)
        o0 += 2 * HID
        b2_sb = qo[0:2, o0:o0 + F]
        o0 += F
        t13 = qo[0:4, o0:o0 + TOK]
        o0 += TOK
        t2 = qo[0:2, o0:o0 + TOK]
        flat = stage[:, :, :].rearrange("p s n -> p (s n)")
        act_t = [flat[:, i * TOK:(i + 1) * TOK] for i in range(2)]
        asum = flat[:, 2 * TOK:5 * TOK].rearrange("p (j t) -> p j t", j=3)
        sig_t = [p_sb[:, NT * F + i * TOK:NT * F + (i + 1) * TOK] for i in range(2)]
        ash = k_hi[:, 0:3 * TOK].rearrange("p (j t) -> p j t", j=3)
        asl = k_lo[:, 0:3 * TOK].rearrange("p (j t) -> p j t", j=3)

        x_loaded = sem("x_loaded")
        small_loaded = sem("small_loaded")
        ident_zeroed = sem("ident_zeroed")
        ident_ready = sem("ident_ready")
        staged = [sem("staged0"), sem("staged1")]
        split_hi = sem("split_hi")
        split_done = sem("split_done")
        ln_step = sem("ln_step")
        var_ready = sem("var_ready")
        std_ready = sem("std_ready")
        xn_ready = sem("xn_ready")
        use_full = sem("use_full")
        use_hi = sem("use_hi")
        use_done = sem("use_done")
        q_spilled = [sem(f"q_spilled{j}") for j in range(4)]
        q_loaded = sem("q_loaded")
        qs_hi_ready = sem("qs_hi_ready")
        qs_ready = sem("qs_ready")
        score_full = sem("score_full")
        max_ready = sem("max_ready")
        exp_ready = sem("exp_ready")
        recip_ready = sem("recip_ready")
        prob_ready = sem("prob_ready")
        tr_full = sem("tr_full")
        tr_hi = sem("tr_hi")
        tr_done = sem("tr_done")
        qo_spilled = sem("qo_spilled")
        o_loaded = [sem(f"o_loaded{j}") for j in range(4)]
        ot_hi_ready = sem("ot_hi_ready")
        ot_ready = sem("ot_ready")
        blk_used = sem("blk_used")
        y_full = sem("y_full")
        gate_ready = sem("gate_ready")
        x1_ready = sem("x1_ready")
        bz_zeroed = sem("bz_zeroed")
        b_loaded = sem("b_loaded")
        a_hi = sem("a_hi")
        a_ready = sem("a_ready")
        t13_full = sem("t13_full")
        t13_ready = sem("t13_ready")
        h_full = sem("h_full")
        h_exp = sem("h_exp")
        ffn_step = sem("ffn_step")
        act_ready = sem("act_ready")
        t2_full = sem("t2_full")
        t2_ready = sem("t2_ready")
        as_hi = sem("as_hi")
        as_ready = sem("as_ready")
        y2_full = sem("y2_full")
        out_ready = sem("out_ready")
        out_stored = sem("out_stored")

        block = es.enter_context(nc.Block())

        def first_use(g, b):
            return MAIN0 + g * GROUP + QUARTERS + b * BODY

        @block.sync
        def _(sp):
            def load(slot, width, src):
                sp.dma_start(stage[:, slot, 0:width], src).then_inc(staged[slot], 16)

            sp.dma_start(x_t, x.rearrange("(t p) n -> p t n", p=TT)).then_inc(x_loaded, 16)
            load(0, W4, wq[0])
            load(1, W4, wq[1])
            sp.dma_start(gates[:, 0:1], gx.partition_broadcast(128)).then_inc(small_loaded, 16)
            sp.dma_start(gates[:, 1:2], gf.partition_broadcast(128)).then_inc(small_loaded, 16)
            sp.dma_start(a13_raw[:, :, :], a13).then_inc(small_loaded, 16)
            sp.dma_start(a2_sb[:, :, :], a2).then_inc(small_loaded, 16)

            def spill_q(k):
                sp.wait_ge(use_done, LN_USES + HEADS4 * (k + 1))
                sp.dma_start(q_dram[k // 4][:, (k % 4) * HEADS4 * TOK:(k % 4 + 1) * HEADS4 * TOK],
                             qo[:, (k % 4) * HEADS4 * TOK:(k % 4 + 1) * HEADS4 * TOK]).then_inc(qo_spilled if k == NG4 - 1 else q_spilled[k % 4], 16)

            for k in range(2, NG4):
                sp.wait_ge(split_done, k - 1)
                load(k % 2, W4, wq[k])
                spill_q(k - 2)
            spill_q(NG4 - 2)
            spill_q(NG4 - 1)

            with sp.Fori(0, G) as g:
                n0 = g * LOADS_G + L_MAIN
                sp.wait_ge(split_done, n0 - 1)
                load(0, W4, wk[g])
                sp.wait_ge(split_done, n0)
                load(1, W4, wv[g])
                for q in range(QUARTERS):
                    sp.wait_ge(split_done, n0 + 1 + q)
                    load(q % 2, NF * PW[q], part(ctx[0], q))
                sp.wait_ge(qo_spilled, (g + 1) * 16)
                for j in range(4):
                    sp.wait_ge(q_spilled[j], (2 if j < 3 else 1) * 16)
                sp.dma_start(qo[:, :], q_dram[g]).then_inc(q_loaded, 16)
                with sp.Fori(1, B) as b:
                    for q in range(QUARTERS):
                        sp.wait_ge(split_done, g * LOADS_G + b * QUARTERS + (L_MAIN + 1 + q))
                        load(q % 2, NF * PW[q], part(ctx[b], q))
                sp.wait_ge(use_done, (g + 1) * GROUP + MAIN0)
                sp.dma_start(o_dram[g], qo[:, :]).then_inc(qo_spilled, 16)

            for k in range(NG4):
                n = L_WO + k
                sp.wait_ge(split_done, n - 1)
                load(n % 2, W4, wo[(k + 4) % NG4])
                if k == 2:
                    sp.wait_ge(qo_spilled, (G + 1) * 16)
                if 2 <= k < 6:
                    sp.wait_ge(ot_ready, k - 1)
                    c = slice((k - 2) * HEADS4 * TOK, (k - 1) * HEADS4 * TOK)
                    sp.dma_start(qo[:, c], o_dram[0][:, c]).then_inc(o_loaded[k - 2], 16)
            for i, (w, width) in enumerate(((w1, HID), (w3, HID), (w2, 3 * F))):
                sp.wait_ge(split_done, L_FFN + i - 1)
                load((L_FFN + i) % 2, width, w)
            sp.dma_start(x_t, x.rearrange("(t p) n -> p t n", p=TT)).then_inc(x_loaded, 16)
            sp.wait_ge(bz_zeroed, 1)
            sp.dma_start(b13_sb[0:2, 0, :], b13[0]).then_inc(b_loaded, 16)
            sp.dma_start(b13_sb[2:4, 1, :], b13[1]).then_inc(b_loaded, 16)
            sp.dma_start(b2_sb, b2).then_inc(b_loaded, 16)
            for t in range(NT):
                sp.wait_ge(out_ready, t + 1)
                sp.dma_start(out[t * TT:(t + 1) * TT, :], x_t[:, t, :]).then_inc(out_stored, 16)
            sp.wait_ge(out_stored, NT * 16)
            sp.wait_ge(small_loaded, 4 * 16)

        @block.gpsimd
        def _(pool):
            nc.gpsimd.memset(ident[:, :], 0.0).then_inc(ident_zeroed, 1)
            pool.wait_ge(ident_zeroed, 1)
            nc.gpsimd.affine_select(out=ident[:, :], in_=ident[:, :], compare_op=ALU.not_equal, fill=1.0,
                                    base=0, pattern=[[-1, 128]], channel_multiplier=1).then_inc(ident_ready, 1)

            def lo_part(n, slot, width, hi, lo):
                pool.wait_ge(split_hi, n + 1)
                nc.gpsimd.tensor_tensor(lo, stage[:, slot, 0:width], hi.bitcast(F32),
                                        ALU.subtract).then_inc(split_done, 1)

            for k in range(NG4):
                s = k % 2
                lo_part(k, s, W4, cx_hi[:, s * W4:(s + 1) * W4], cx_lo[:, s * W4:(s + 1) * W4])
            with pool.Fori(0, G) as g:
                n0 = g * LOADS_G + L_MAIN
                lo_part(n0, 0, W4, wk_hi[:, :], wk_lo[:, :])
                lo_part(n0 + 1, 1, W4, wv_hi[:, :], wv_lo[:, :])
                with pool.Fori(0, B) as b:
                    for q in range(QUARTERS):
                        lo_part(g * LOADS_G + b * QUARTERS + (L_MAIN + 2 + q), q % 2, NF * PW[q],
                                part(cx_hi, q), part(cx_lo, q))
            for k in range(NG4):
                s = k % 2
                lo_part(L_WO + k, s, W4, cx_hi[:, s * W4:(s + 1) * W4], cx_lo[:, s * W4:(s + 1) * W4])
            lo_part(L_FFN, 0, HID, w1h, w1l)
            lo_part(L_FFN + 1, 1, HID, w3h, w3l)
            lo_part(L_FFN + 2, 0, 3 * F, v_hi[:, HID:HID + 3 * F], v_lo[:, HID:HID + 3 * F])

        @block.scalar
        def _(act):
            copy = ACT.Copy

            def hi_part(n, slot, turn, width, hi):
                act.wait_ge(staged[slot], (turn + 1) * 16)
                nc.scalar.activation(hi, stage[:, slot, 0:width], copy).then_inc(split_hi, 1)

            def take(n, dst, src):
                act.wait_ge(use_full, n + 1)
                nc.scalar.activation(dst, src, copy).then_inc(use_hi, 1)

            def layernorm_std(i):
                act.wait_ge(var_ready, i + 1)
                nc.scalar.activation(std[0:TT, :], std[0:TT, :], ACT.Sqrt).then_inc(std_ready, 1)

            layernorm_std(0)
            hi_part(0, 0, 0, W4, cx_hi[:, 0:W4])
            hi_part(1, 1, 0, W4, cx_hi[:, W4:2 * W4])
            for f in range(NF):
                take(f, xT[:, 0, f, :], ring[f % 2][:, 0:TOK])
            for k in range(NG4):
                for j in range(HEADS4):
                    n = LN_USES + k * HEADS4 + j
                    if k >= 4 and j == 0:
                        act.wait_ge(q_spilled[k % 4], 16)
                    h = (k % 4) * HEADS4 + j
                    act.wait_ge(use_full, n + 1)
                    nc.scalar.activation(qo[:, h * TOK:(h + 1) * TOK], ring[n % 2][:, 0:TOK], copy,
                                         scale=SCALE).then_inc(use_done, 1)
                if k + 2 < NG4:
                    s = k % 2
                    hi_part(k + 2, s, (k + 2) // 2, W4, cx_hi[:, s * W4:(s + 1) * W4])

            def k_use(n, bank, q):
                take(n, k_hi[:, P0[q]:P0[q] + PW[q]], ring[bank][:, 0:PW[q]])

            def v_use(n, bank, c):
                take(n, vh[0:CH, c, :], ring[bank][0:CH, 0:VW])

            def o_use(n, bank):
                take(n, otmp[:, :], ring[bank][:, 2 * ROWS:4 * ROWS])

            def exp_half(step, h):
                act.wait_ge(max_ready, step * 2 + h + 1)
                nc.scalar.activation(ph[0:ROWS, h, :].rearrange("p (t n) -> p t n", t=THIRDS),
                                     banks[0:ROWS, 3 * h:3 * h + 3, 0:T3], ACT.Exp, bias=negmax[0:ROWS, h:h + 1],
                                     accum_out=psum_row[0:ROWS, h:h + 1]).then_inc(exp_ready, 1)

            def transposed(step):
                for j in range(NPT):
                    act.wait_ge(tr_full, step * NPT + j + 1)
                    for h in range(2):
                        ins = nc.scalar.activation(
                            pt6[0:CH, j, :, 0, h, :],
                            banks[0:CH, 3 * h + j, 0:CPB * ROWS].rearrange("p (c r) -> p c r", c=CPB), copy)
                    ins.then_inc(tr_hi, 1)

            def body(g, b, last):
                u = first_use(g, b)
                step = (g * B + b) * PAIRS
                nc.scalar.activation(qsh3, qo3[:, :, bass.ts(b, TQ)], copy).then_inc(qs_hi_ready, 1)
                for c in range(V_USES):
                    v_use(u + c, c % 2, c)
                for p in (0, 1):
                    k0 = U_K[p + 1]
                    exp_half(step + p, 0)
                    k_use(u + k0, k0 % 2, 0)
                    exp_half(step + p, 1)
                    k_use(u + k0 + 1, (k0 + 1) % 2, 1)
                    k_use(u + k0 + 2, k0 % 2, 2)
                    transposed(step + p)
                    k_use(u + k0 + 3, (k0 + 1) % 2, 3)
                    o_use(u + U_O[p], U_O[p] % 2)
                for q in range(QUARTERS):
                    n = U_KV + q + PC0[q]
                    if q == 0:
                        exp_half(step + 2, 0)
                    if q == 3:
                        transposed(step + 2)
                    k_use(u + n, n % 2, q)
                    if q == 0:
                        exp_half(step + 2, 1)
                    for c in range(PCH[q]):
                        v_use(u + n + 1 + c, (n + 1 + c) % 2, PC0[q] + c)
                    if not last:
                        m = (g * LOADS_G + (b + 1) * QUARTERS + (L_MAIN + 2 + q))
                        hi_part(m, q % 2, g * (LOADS_G // 2) + (b + 1) * 2 + (L_MAIN // 2 + 1 + q // 2), NF * PW[q], part(cx_hi, q))
                exp_half(step + 3, 0)
                exp_half(step + 3, 1)
                o_use(u + U_O[2], U_O[2] % 2)
                if not last:
                    for q in range(3):
                        k_use(u + U_K0 + q, (U_K0 + q) % 2, q)
                transposed(step + 3)
                if not last:
                    k_use(u + U_K0 + 3, (U_K0 + 3) % 2, 3)
                    o_use(u + U_O[3], U_O[3] % 2)
                else:
                    o_use(u + U_O[3] - QUARTERS, U_O[3] % 2)

            with act.Fori(0, G) as g:
                t0 = g * (LOADS_G // 2) + L_MAIN // 2
                hi_part(g * LOADS_G + L_MAIN, 0, t0, W4, wk_hi[:, :])
                hi_part(g * LOADS_G + L_MAIN + 1, 1, t0, W4, wv_hi[:, :])
                for q in range(QUARTERS):
                    hi_part(g * LOADS_G + (L_MAIN + 2 + q), q % 2, t0 + 1 + q // 2, NF * PW[q], part(cx_hi, q))
                for q in range(QUARTERS):
                    k_use(first_use(g, 0) - QUARTERS + q, q % 2, q)
                act.wait_ge(q_loaded, (g + 1) * 16)
                with act.Fori(0, B - 1) as b:
                    body(g, b, False)
                body(g, B - 1, True)

            act.wait_ge(small_loaded, 4 * 16)
            nc.scalar.activation(tgate[:, :], gates[:, :], ACT.Tanh).then_inc(gate_ready, 1)
            nc.scalar.activation(a13_hi[:, :, :], a13_raw[:, :, :], copy).then_inc(a_hi, 1)
            for k in range(NG4):
                n, s = L_WO + k, k % 2
                if k >= 2:
                    act.wait_ge(blk_used, k - 1)
                hi_part(n, s, n // 2, W4, cx_hi[:, s * W4:(s + 1) * W4])
                if k >= 4:
                    act.wait_ge(o_loaded[k - 4], 16)
                nc.scalar.activation(ot_hi[s], qo[:, (k % 4) * HEADS4 * TOK:(k % 4 + 1) * HEADS4 * TOK],
                                     copy).then_inc(ot_hi_ready, 1)
            hi_part(L_FFN, 0, L_FFN // 2, HID, w1h)
            hi_part(L_FFN + 1, 1, L_FFN // 2, HID, w3h)
            hi_part(L_FFN + 2, 0, L_FFN // 2 + 1, 3 * F, v_hi[:, HID:HID + 3 * F])
            layernorm_std(1)
            for f in range(NF + 1):
                take(END + f, xT[:, 0, f, :], ring[f % 2][:, 0:TOK])
            act.wait_ge(t13_full, 1)
            nc.scalar.activation(t13, ring[1][0:4, 0:TOK], copy, scale=LORA).then_inc(t13_ready, 1)
            for c, (_, n, _) in enumerate(HCH):
                act.wait_ge(h_full, c + 1)
                if c >= 2:
                    act.wait_ge(act_ready, c - 1)
                nc.scalar.activation(sig_t[c % 2][0:n, :], banks[0:n, c % 2, 0:TOK], ACT.Exp,
                                     scale=-1.0).then_inc(h_exp, 1)
            act.wait_ge(t2_full, 1)
            nc.scalar.activation(t2, ring[0][0:2, 0:TOK], copy, scale=LORA).then_inc(t2_ready, 1)
            act.wait_ge(act_ready, len(HCH))
            for j, (_, n) in enumerate(HCUT):
                nc.scalar.activation(ash[0:n, j, :], asum[0:n, j, :], copy).then_inc(as_hi, 1)

        @block.vector
        def _(dve):
            def rest(n, dst, src, hi, skipped=Q_USES):
                dve.wait_ge(use_hi, n + 1 - skipped)
                nc.vector.tensor_tensor(dst, src, hi.bitcast(F32), ALU.subtract).then_inc(use_done, 1)

            def layernorm(i, xs):
                for t in range(NT):
                    nc.vector.bn_stats(stats[0:TT, t, :], x_t[:, t, :]).then_inc(ln_step, 1)
                for t in range(NT):
                    dve.wait_ge(ln_step, step_of[0] + t + 1)
                    nc.vector.bn_aggr(mv[0:TT, t, :], stats[0:TT, t, :]).then_inc(ln_step, 1)
                dve.wait_ge(ln_step, step_of[0] + 2 * NT)
                nc.vector.tensor_scalar(std[0:TT, :], mv[0:TT, :, 1], EPS, None, ALU.add).then_inc(var_ready, 1)
                dve.wait_ge(std_ready, i + 1)
                nc.vector.reciprocal(rstd[0:TT, :], std[0:TT, :]).then_inc(ln_step, 1)
                dve.wait_ge(ln_step, step_of[0] + 2 * NT + 1)
                for t in range(NT):
                    ins = nc.vector.tensor_scalar(xn_t[:, t, 0:F], x_t[:, t, :], mv[0:TT, t, 0:1], rstd[0:TT, t:t + 1],
                                                  ALU.subtract, ALU.mult)
                    if not xs:
                        ins.then_inc(xn_ready, 1)
                        continue
                    ins.then_inc(ln_step, 1)
                step_of[0] += 2 * NT + 1

            step_of = [0]
            dve.wait_ge(x_loaded, 16)
            layernorm(0, False)
            for f in range(NF):
                rest(f, xT[:, 1, f, :], ring[f % 2][:, 0:TOK], xT[:, 0, f, :], skipped=0)
            def k_use(n, bank, q):
                c = slice(P0[q], P0[q] + PW[q])
                rest(n, k_lo[:, c], ring[bank][:, 0:PW[q]], k_hi[:, c])

            def v_use(n, bank, c):
                rest(n, vl[0:CH, c, :], ring[bank][0:CH, 0:VW], vh[0:CH, c, :])

            def o_use(n, bank, b, p, skipped=Q_USES):
                dve.wait_ge(use_hi, n + 1 - skipped)
                nc.vector.tensor_tensor(qo3[:, p * REP:(p + 1) * REP, bass.ts(b, TQ)],
                                        ring[bank][:, 0:2 * ROWS].rearrange("p (h t) -> p h t", h=REP),
                                        otmp[:, :].rearrange("p (h t) -> p h t", h=REP),
                                        ALU.add).then_inc(use_done, 1)

            def max_half(step, h):
                dve.wait_ge(score_full, step * 2 + h + 1)
                nc.vector.tensor_reduce(negmax[0:ROWS, h:h + 1], banks[0:ROWS, 3 * h:3 * h + 3, 0:T3], AX.XY,
                                        ALU.max, negate=True).then_inc(max_ready, 1)

            def normalise(step, h):
                n = step * 2 + h + 1
                dve.wait_ge(exp_ready, n)
                nc.vector.reciprocal(rinv[0:ROWS, h:h + 1], psum_row[0:ROWS, h:h + 1]).then_inc(recip_ready, 1)
                dve.wait_ge(recip_ready, n)
                nc.vector.tensor_scalar(ph[0:ROWS, h, :], ph[0:ROWS, h, :], rinv[0:ROWS, h:h + 1], None,
                                        ALU.mult).then_inc(prob_ready, 1)

            def transposed(step):
                for j in range(NPT):
                    dve.wait_ge(tr_hi, step * NPT + j + 1)
                    for h in range(2):
                        ins = nc.vector.tensor_tensor(
                            pt6[0:CH, j, :, 1, h, :],
                            banks[0:CH, 3 * h + j, 0:CPB * ROWS].rearrange("p (c r) -> p c r", c=CPB),
                            pt6[0:CH, j, :, 0, h, :].bitcast(F32), ALU.subtract)
                    ins.then_inc(tr_done, 1)

            def body(g, b, last):
                u = first_use(g, b)
                step = (g * B + b) * PAIRS
                dve.wait_ge(qs_hi_ready, g * B + b + 1)
                nc.vector.tensor_tensor(qsl3, qo3[:, :, bass.ts(b, TQ)], qsh3.bitcast(F32),
                                        ALU.subtract).then_inc(qs_ready, 1)
                for c in range(V_USES):
                    v_use(u + c, c % 2, c)
                for p in (0, 1):
                    k0 = U_K[p + 1]
                    max_half(step + p, 0)
                    max_half(step + p, 1)
                    normalise(step + p, 0)
                    k_use(u + k0, k0 % 2, 0)
                    normalise(step + p, 1)
                    k_use(u + k0 + 1, (k0 + 1) % 2, 1)
                    k_use(u + k0 + 2, k0 % 2, 2)
                    transposed(step + p)
                    k_use(u + k0 + 3, (k0 + 1) % 2, 3)
                    o_use(u + U_O[p], U_O[p] % 2, b, p)
                max_half(step + 2, 0)
                max_half(step + 2, 1)
                for q in range(QUARTERS):
                    n = U_KV + q + PC0[q]
                    if q == 0:
                        normalise(step + 2, 0)
                    if q == 3:
                        transposed(step + 2)
                    k_use(u + n, n % 2, q)
                    if q == 0:
                        normalise(step + 2, 1)
                    for c in range(PCH[q]):
                        v_use(u + n + 1 + c, (n + 1 + c) % 2, PC0[q] + c)
                max_half(step + 3, 0)
                max_half(step + 3, 1)
                normalise(step + 3, 0)
                normalise(step + 3, 1)
                o_use(u + U_O[2], U_O[2] % 2, b, 2)
                if not last:
                    for q in range(3):
                        k_use(u + U_K0 + q, (U_K0 + q) % 2, q)
                transposed(step + 3)
                if not last:
                    k_use(u + U_K0 + 3, (U_K0 + 3) % 2, 3)
                    o_use(u + U_O[3], U_O[3] % 2, b, 3)
                else:
                    o_use(u + U_O[3] - QUARTERS, U_O[3] % 2, b, 3)

            with dve.Fori(0, G) as g:
                for q in range(QUARTERS):
                    k_use(first_use(g, 0) - QUARTERS + q, q % 2, q)
                with dve.Fori(0, B - 1) as b:
                    body(g, b, False)
                body(g, B - 1, True)

            dve.wait_ge(a_hi, 1)
            nc.vector.tensor_tensor(a13_lo[:, :, :], a13_raw[:, :, :], a13_hi[:, :, :].bitcast(F32),
                                    ALU.subtract).then_inc(a_ready, 1)
            for k in range(NG4):
                dve.wait_ge(ot_hi_ready, k + 1)
                nc.vector.tensor_tensor(ot_lo[k % 2], qo[:, (k % 4) * HEADS4 * TOK:(k % 4 + 1) * HEADS4 * TOK],
                                        ot_hi[k % 2].bitcast(F32), ALU.subtract).then_inc(ot_ready, 1)
            dve.wait_ge(ot_ready, NG4)
            nc.vector.memset(b13_sb, 0.0).then_inc(bz_zeroed, 1)
            dve.wait_ge(gate_ready, 1)
            dve.wait_ge(x_loaded, 2 * 16)
            for t in range(NT):
                dve.wait_ge(y_full, t + 1)
                nc.vector.scalar_tensor_tensor(x_t[:, t, :], banks[0:TT, t, :], tgate[0:TT, 0:1], x_t[:, t, :],
                                               ALU.mult, ALU.add).then_inc(x1_ready, 1)
            dve.wait_ge(x1_ready, NT)
            layernorm(1, True)
            dve.wait_ge(ln_step, step_of[0] + NT)
            for t in range(NT):
                nc.vector.tensor_reduce(xn_t[:, t, F:F + 128], xn_t[:, t, 0:F].rearrange("p (f n) -> p n f", f=NF),
                                        AX.X, ALU.add).then_inc(xn_ready, 1)
            for f in range(NF + 1):
                rest(END + f, xT[:, 1, f, :], ring[f % 2][:, 0:TOK], xT[:, 0, f, :])
            step = 0
            dve.wait_ge(split_done, L_FFN + 3)
            for c, (_, n, j) in enumerate(HCH):
                sg = sig_t[c % 2][0:n, :]
                ac = act_t[c % 2][0:n, :]
                dve.wait_ge(h_exp, c + 1)
                nc.vector.tensor_scalar(sg, sg, 1.0, None, ALU.add).then_inc(ffn_step, 1)
                dve.wait_ge(ffn_step, step + 1)
                nc.vector.reciprocal(sg, sg).then_inc(ffn_step, 1)
                dve.wait_ge(ffn_step, step + 2)
                nc.vector.tensor_tensor(sg, banks[0:n, c % 2, 0:TOK], sg, ALU.mult).then_inc(ffn_step, 1)
                dve.wait_ge(ffn_step, step + 3)
                nc.vector.tensor_tensor(ac, banks[0:n, 2 + c % 2, 0:TOK], sg, ALU.mult).then_inc(ffn_step, 1)
                dve.wait_ge(ffn_step, step + 4)
                step += 4
                if c < 3:
                    nc.vector.tensor_copy(asum[0:n, j, :], ac).then_inc(act_ready, 1)
                else:
                    nc.vector.tensor_tensor(asum[0:n, j, :], asum[0:n, j, :], ac, ALU.add).then_inc(act_ready, 1)
            for j, (_, n) in enumerate(HCUT):
                dve.wait_ge(as_hi, j + 1)
                nc.vector.tensor_tensor(asl[0:n, j, :], asum[0:n, j, :], ash[0:n, j, :].bitcast(F32),
                                        ALU.subtract).then_inc(as_ready, 1)
            for t in range(NT):
                dve.wait_ge(y2_full, t + 1)
                nc.vector.scalar_tensor_tensor(x_t[:, t, :], banks[0:TT, t, :], tgate[0:TT, 1:2], x_t[:, t, :],
                                               ALU.mult, ALU.add).then_inc(out_ready, 1)

        @block.tensor
        def _(pe):
            def three(dst, ah, al, bh, bl, first, last):
                nc.tensor.matmul(dst, ah, bh, start=first, stop=False)
                nc.tensor.matmul(dst, ah, bl, start=False, stop=False)
                return nc.tensor.matmul(dst, al, bh, start=False, stop=last)

            def bank_free(n):
                pe.wait_ge(use_done, n - 1)

            def transposes(n0, nf):
                for f in range(nf):
                    if n0 + f >= 2:
                        bank_free(n0 + f)
                    for t in range(NT):
                        ins = nc.tensor.transpose(ring[f % 2][:, t * TT:(t + 1) * TT],
                                                  xn_t[:, t, f * 128:(f + 1) * 128], ident[0:TT, 0:TT])
                    ins.then_inc(use_full, 1)

            pe.wait_ge(ident_ready, 1)
            pe.wait_ge(xn_ready, NT)
            transposes(0, NF)
            pe.wait_ge(use_done, LN_USES)
            for k in range(NG4):
                pe.wait_ge(split_done, k + 1)
                wh, wl = blk_hi[k % 2], blk_lo[k % 2]
                for j in range(HEADS4):
                    n = LN_USES + k * HEADS4 + j
                    bank_free(n)
                    for f in range(NF):
                        ins = three(ring[n % 2][:, 0:TOK], wh[:, f, j * D:(j + 1) * D], wl[:, f, j * D:(j + 1) * D],
                                    xT[:, 0, f, :], xT[:, 1, f, :], f == 0, f == NF - 1)
                    ins.then_inc(use_full, 1)

            def k_use(n, bank, p, q):
                bank_free(n)
                c = slice(p * D, (p + 1) * D)
                for f in range(NF):
                    ins = three(ring[bank][:, 0:PW[q]], wkh[:, f, c], wkl[:, f, c], cxh[q][:, f, :], cxl[q][:, f, :],
                                f == 0, f == NF - 1)
                ins.then_inc(use_full, 1)

            def v_use(n, bank, s, c):
                bank_free(n)
                q = max(i for i in range(QUARTERS) if PC0[i] <= c)
                i = slice((c - PC0[q]) * CH, (c - PC0[q] + 1) * CH)
                for f in range(NF):
                    ins = three(ring[bank][0:CH, 0:VW], cxh[q][:, f, i], cxl[q][:, f, i],
                                wvh[:, f, s * VW:(s + 1) * VW], wvl[:, f, s * VW:(s + 1) * VW], f == 0, f == NF - 1)
                ins.then_inc(use_full, 1)

            def scores(p, keys_done):
                pe.wait_ge(use_done, keys_done)
                for h in range(2):
                    r = slice((p * REP + 2 * h) * TQ, (p * REP + 2 * h) * TQ + ROWS)
                    for t in range(THIRDS):
                        c = slice(t * T3, (t + 1) * T3)
                        ins = three(banks[0:ROWS, 3 * h + t, 0:T3], qs_hi[:, r], qs_lo[:, r], k_hi[:, c], k_lo[:, c],
                                    True, True)
                    ins.then_inc(score_full, 1)

            def transpose_probs(step):
                for j in range(NPT):
                    for h in range(2):
                        if j == 0:
                            pe.wait_ge(prob_ready, step * 2 + h + 1)
                        for c in range(CPB):
                            at = (j * CPB + c) * CH
                            ins = nc.tensor.transpose(banks[0:CH, 3 * h + j, c * ROWS:(c + 1) * ROWS],
                                                      ph[0:ROWS, h, at:at + CH], ident[0:ROWS, 0:ROWS])
                    ins.then_inc(tr_full, 1)

            def weigh(n, bank, step, p):
                bank_free(n)
                i = slice(p % 2 * D, (p % 2 + 1) * D)
                for c in range(NCH):
                    if c % CPB == 0:
                        pe.wait_ge(tr_done, step * NPT + c // CPB + 1)
                    if c > 0:
                        nc.tensor.matmul(ring[bank][:, 0:2 * ROWS], vl[0:CH, c, i], pt3[0:CH, c, 0:2 * ROWS],
                                         start=False, stop=False)
                    ins = nc.tensor.matmul(ring[bank][:, 0:4 * ROWS], vh[0:CH, c, i], pt3[0:CH, c, :],
                                           start=(c == 0), stop=(c == NCH - 1))
                    if c == 0:
                        nc.tensor.matmul(ring[bank][:, 0:2 * ROWS], vl[0:CH, c, i], pt3[0:CH, c, 0:2 * ROWS],
                                         start=False, stop=False)
                ins.then_inc(use_full, 1)

            def body(g, b, last):
                u = first_use(g, b)
                step = (g * B + b) * PAIRS
                for c in range(V_USES):
                    v_use(u + c, c % 2, 0, c)
                pe.wait_ge(qs_ready, g * B + b + 1)
                for p in (0, 1):
                    k0 = U_K[p + 1]
                    scores(p, u + k0)
                    for q in range(3):
                        k_use(u + k0 + q, (k0 + q) % 2, p + 1, q)
                    transpose_probs(step + p)
                    k_use(u + k0 + 3, (k0 + 3) % 2, p + 1, 3)
                    weigh(u + U_O[p], U_O[p] % 2, step + p, p)
                scores(2, u + U_KV - 1)
                for q in range(QUARTERS):
                    n = U_KV + q + PC0[q]
                    if q == 3:
                        transpose_probs(step + 2)
                    k_use(u + n, n % 2, 3, q)
                    for c in range(PCH[q]):
                        v_use(u + n + 1 + c, (n + 1 + c) % 2, 1, PC0[q] + c)
                pe.wait_ge(tr_done, (step + 3) * NPT)
                scores(3, u + U_KV + 3 + PC0[3] + 1)
                pe.wait_ge(use_done, u + U_O[2])
                weigh(u + U_O[2], U_O[2] % 2, step + 2, 2)
                if not last:
                    n1 = g * LOADS_G + (b + 1) * QUARTERS + (L_MAIN + 2)
                    for q in range(3):
                        pe.wait_ge(split_done, n1 + q + 1)
                        k_use(u + U_K0 + q, (U_K0 + q) % 2, 0, q)
                transpose_probs(step + 3)
                if not last:
                    pe.wait_ge(split_done, n1 + 4)
                    k_use(u + U_K0 + 3, (U_K0 + 3) % 2, 0, 3)
                    weigh(u + U_O[3], U_O[3] % 2, step + 3, 3)
                else:
                    weigh(u + U_O[3] - QUARTERS, U_O[3] % 2, step + 3, 3)

            with pe.Fori(0, G) as g:
                for q in range(QUARTERS):
                    pe.wait_ge(split_done, g * LOADS_G + (L_MAIN + 2 + q + 1))
                    k_use(first_use(g, 0) - QUARTERS + q, q % 2, 0, q)
                with pe.Fori(0, B - 1) as b:
                    body(g, b, False)
                body(g, B - 1, True)

            pe.wait_ge(tr_done, G * B * PAIRS * NPT)
            for k in range(NG4):
                pe.wait_ge(split_done, L_WO + k + 1)
                pe.wait_ge(ot_ready, k + 1)
                wh, wl = blk_hi[k % 2], blk_lo[k % 2]
                for j in range(HEADS4):
                    for t in range(NT):
                        c = slice(j * TOK + t * TT, j * TOK + (t + 1) * TT)
                        first, last = k == 0 and j == 0, k == NG4 - 1 and j == HEADS4 - 1
                        ins = three(banks[0:TT, t, :], ot_hi[k % 2][:, c], ot_lo[k % 2][:, c], wh[:, j, :], wl[:, j, :],
                                    first, last)
                        if last:
                            ins.then_inc(y_full, 1)
                if k < NG4 - 1:
                    ins.then_inc(blk_used, 1)
            pe.wait_ge(xn_ready, 2 * NT)
            transposes(END, NF + 1)
            pe.wait_ge(a_ready, 1)
            pe.wait_ge(use_done, END + NF + 1)
            for f in range(NF):
                ins = three(ring[1][0:4, 0:TOK], a13_hi[:, f, :], a13_lo[:, f, :], xT[:, 0, f, :], xT[:, 1, f, :],
                            f == 0, f == NF - 1)
            ins.then_inc(t13_full, 1)
            pe.wait_ge(split_done, L_FFN + 3)
            pe.wait_ge(small_loaded, 4 * 16)
            pe.wait_ge(b_loaded, 3 * 16)
            pe.wait_ge(t13_ready, 1)

            def lora_down(c):
                n = HCH[c][1]
                pe.wait_ge(act_ready, c + 1)
                return nc.tensor.matmul(ring[0][0:2, 0:TOK], a2_sb[0:n, c, :], act_t[c % 2][0:n, :],
                                        start=(c == 0), stop=(c == len(HCH) - 1))

            for c, (at, n, _) in enumerate(HCH):
                if c >= 2:
                    lora_down(c - 2)
                hid = slice(at, at + n)
                for i, (wh, wl) in enumerate(((w1h, w1l), (w3h, w3l))):
                    dst = banks[0:n, 2 * i + c % 2, 0:TOK]
                    three(dst, wh[:, hid], wl[:, hid], xT[:, 0, NF, :], xT[:, 1, NF, :], True, False)
                    ins = nc.tensor.matmul(dst, b13_sb[:, i, hid], t13, start=False, stop=True)
                ins.then_inc(h_full, 1)
            lora_down(len(HCH) - 2)
            lora_down(len(HCH) - 1).then_inc(t2_full, 1)
            pe.wait_ge(t2_ready, 1)
            pe.wait_ge(as_ready, 3)
            for t in range(NT):
                c = slice(t * TT, (t + 1) * TT)
                for j, (_, n) in enumerate(HCUT):
                    three(banks[0:TT, t, :], ash[0:n, j, c], asl[0:n, j, c], w2h[0:n, j, :], w2l[0:n, j, :],
                          j == 0, False)
                nc.tensor.matmul(banks[0:TT, t, :], t2[:, c], b2_sb, start=False, stop=True).then_inc(y2_full, 1)


def kernel(x, ctx_4096, g_xattn, g_ffn, L0_xattn_wq, L0_xattn_wk, L0_xattn_wv, L0_xattn_wo, L0_ffn_w1q,
           L0_ffn_a1, L0_ffn_b1, L0_ffn_w3q, L0_ffn_a3, L0_ffn_b3, L0_ffn_w2q, L0_ffn_a2, L0_ffn_b2):
    import numpy as np
    import concourse.bacc as bacc
    from concourse.bass_utils import run_bass_kernel_spmd as run

    c = np.ascontiguousarray

    def blocks(w, n):
        w = np.asarray(w)
        return c(w.reshape(NF, 128, n, -1).transpose(2, 1, 0, 3).reshape(n, 128, -1))

    ctx = np.asarray(ctx_4096).reshape(B, TK, NF, 128).transpose(0, 3, 2, 1)
    ctx = np.concatenate([ctx[..., P0[q]:P0[q] + PW[q]].reshape(B, 128, -1) for q in range(QUARTERS)], -1)
    w2t = np.zeros((3 * 128, F), np.float32)
    w2t[:HQR] = np.asarray(L0_ffn_w2q).T
    a2t = np.zeros((128, len(HCH), 2), np.float32)
    for i, (at, n, _) in enumerate(HCH):
        a2t[:n, i] = np.asarray(L0_ffn_a2)[:, at:at + n].T
    a13 = np.concatenate([np.asarray(L0_ffn_a1), np.asarray(L0_ffn_a3)], 0)
    arrays = {
        "x": c(np.asarray(x).reshape(TOK, F)),
        "ctx": c(ctx),
        "gx": c(np.asarray(g_xattn)[:1]),
        "gf": c(np.asarray(g_ffn)[:1]),
        "wq": blocks(L0_xattn_wq, NG4),
        "wk": blocks(L0_xattn_wk, G),
        "wv": blocks(L0_xattn_wv, G),
        "wo": c(np.asarray(L0_xattn_wo).reshape(NG4, HEADS4, D, F).transpose(0, 2, 1, 3).reshape(NG4, 128, -1)),
        "w1": c(np.asarray(L0_ffn_w1q).T),
        "w3": c(np.asarray(L0_ffn_w3q).T),
        "w2": c(w2t.reshape(3, 128, F).transpose(1, 0, 2).reshape(128, 3 * F)),
        "a13": c(a13.T.reshape(NF, 128, 4).transpose(1, 0, 2)),
        "a2": a2t,
        "b13": c(np.stack([np.asarray(L0_ffn_b1).T, np.asarray(L0_ffn_b3).T])),
        "b2": c(np.asarray(L0_ffn_b2).T),
    }
    nc = bacc.Bacc("TRN2", target_bir_lowering=False, num_devices=1)
    args = [nc.dram_tensor(n, a.shape, mybir.dt.from_np(a.dtype), kind="ExternalInput").ap() for n, a in arrays.items()]
    out = nc.dram_tensor("out", (TOK, F), F32, kind="ExternalOutput").ap()
    q_dram = nc.dram_tensor("q_dram", (G, 128, GH * TOK), F32).ap()
    o_dram = nc.dram_tensor("o_dram", (G, 128, GH * TOK), F32).ap()
    flamingo_kernel(nc, *args, out, q_dram, o_dram)
    r = run(nc, [arrays], core_ids=[0])
    return r.results[0]["out"].reshape(B, TQ, F)
```

```python
from contextlib import ExitStack

import concourse.bass as bass
from concourse import mybir

F32 = mybir.dt.float32
F32R = mybir.dt.float32r
ALU = mybir.AluOpType
ACT = mybir.ActivationFunctionType
AX = mybir.AxisListType

B, TQ, F = 8, 56, 512
TK = 1500
HQ, HKV, D = 32, 8, 128
REP = HQ // HKV
HID = 1376
EPS = 1e-5
SCALE = 1.0 / float(D) ** 0.5
LORA = 0.5

NF = F // 128
TOK = B * TQ
TT = 112
NT = TOK // TT
G = 2
PAIRS = HKV // G
GH = HQ // G
QUARTERS = 4
CH = 125
NCH = TK // CH
PCH = (2, 4, 2, 4)
PC0 = tuple(sum(PCH[:q]) for q in range(QUARTERS))
PW = tuple(n * CH for n in PCH)
P0 = tuple(n * CH for n in PC0)
THIRDS = 3
T3 = TK // THIRDS
ROWS = 2 * TQ
CPB = 4
NPT = NCH // CPB
VW = 2 * D
HEADS4 = 4
NG4 = HQ // HEADS4
W4 = NF * HEADS4 * D

HQR = HID // 4
HCUT = [(0, 128), (128, 128), (256, HQR - 256)]
HCH = [(q * HQR + o, n, j) for q in range(4) for j, (o, n) in enumerate(HCUT)]

LN_USES = NF
Q_USES = HQ
V_USES = NCH
BODY = 2 * V_USES + PAIRS * (QUARTERS + 1)
MAIN0 = LN_USES + Q_USES
END = MAIN0 + G * B * BODY
U_V01 = 0
U_K = {1: V_USES, 2: V_USES + 5}
U_O = {0: V_USES + 4, 1: V_USES + 9, 2: V_USES + 10 + 16, 3: V_USES + 10 + 17 + 4}
U_KV = V_USES + 10
U_K0 = V_USES + 10 + 17
L_WK = NG4
L_CTX0 = L_WK + 1
L_WV = L_CTX0 + QUARTERS
L_LOOP = [L_WV + 1]
L_SWITCH = L_LOOP[0] + (B - 1) * QUARTERS
L_LOOP.append(L_SWITCH + QUARTERS + 2)
L_WO = L_LOOP[1] + (B - 1) * QUARTERS
L_FFN = L_WO + NG4
NEXT_BATCH, NEXT_GROUP, LAST = range(3)


def flamingo_kernel(nc, x, ctx, gx, gf, wq, wk, wv, wo, w1, w3, w2, a13, a2, b13, b2, out, q_dram, o_dram):
    es = ExitStack()
    with es:
        def sb(name, shape, dt=F32):
            return es.enter_context(nc.sbuf_tensor(name, shape, dt))

        def sem(name):
            return es.enter_context(nc.semaphore(name))

        stage = sb("stage", [128, 2, W4])
        wk_hi = sb("wk_hi", [128, W4], F32R)
        wk_lo = sb("wk_lo", [128, W4], F32R)
        wv_hi = sb("wv_hi", [128, W4], F32R)
        wv_lo = sb("wv_lo", [128, W4], F32R)
        cx_hi = sb("cx_hi", [128, NF * TK], F32R)
        cx_lo = sb("cx_lo", [128, NF * TK], F32R)
        v_hi = sb("v_hi", [128, NCH * VW], F32R)
        v_lo = sb("v_lo", [128, NCH * VW], F32R)
        k_hi = sb("k_hi", [128, TK], F32R)
        k_lo = sb("k_lo", [128, TK], F32R)
        qo = sb("qo", [128, GH * TOK])
        qs_hi = sb("qs_hi", [128, GH * TQ], F32R)
        qs_lo = sb("qs_lo", [128, GH * TQ], F32R)
        p_sb = sb("p_sb", [128, 2 * TK])
        pt = sb("pt", [128, NPT * CPB * 4 * ROWS], F32R)
        otmp = sb("otmp", [128, 2 * ROWS])
        ident = sb("ident", [128, 128])
        negmax = sb("negmax", [128, 2])
        psum_row = sb("psum_row", [128, 2])
        rinv = sb("rinv", [128, 2])
        stats = sb("stats", [128, NT, 6])
        mv = sb("mv", [128, NT, 2])
        std = sb("std", [128, NT])
        rstd = sb("rstd", [128, NT])
        gates = sb("gates", [128, 2])
        tgate = sb("tgate", [128, 2])
        a13_raw = sb("a13_raw", [128, NF, 4])
        a13_hi = sb("a13_hi", [128, NF, 4], F32R)
        a13_lo = sb("a13_lo", [128, NF, 4], F32R)
        a2_sb = sb("a2_sb", [128, len(HCH), 2])

        banks = es.enter_context(nc.psum_tensor("banks", [128, 8, 512], F32))
        ring = [banks[:, 6, :], banks[:, 7, :]]

        def w4(t):
            return t[:, 0:W4].rearrange("p (f n) -> p f n", f=NF)
        wkh, wkl, wvh, wvl = w4(wk_hi), w4(wk_lo), w4(wv_hi), w4(wv_lo)

        def part(t, q):
            return t[:, NF * P0[q]:NF * (P0[q] + PW[q])]

        cxh = [part(cx_hi, q).rearrange("p (f t) -> p f t", f=NF) for q in range(QUARTERS)]
        cxl = [part(cx_lo, q).rearrange("p (f t) -> p f t", f=NF) for q in range(QUARTERS)]
        vh = v_hi[:, :].rearrange("p (c n) -> p c n", c=NCH)
        vl = v_lo[:, :].rearrange("p (c n) -> p c n", c=NCH)
        qo3 = qo[:, :].rearrange("p (h t) -> p h t", h=GH)
        qsh3 = qs_hi[:, :].rearrange("p (h t) -> p h t", h=GH)
        qsl3 = qs_lo[:, :].rearrange("p (h t) -> p h t", h=GH)
        ph = p_sb[:, :].rearrange("p (h t) -> p h t", h=2)
        pt6 = pt[:, :].rearrange("p (g c s h r) -> p g c s h r", g=NPT, c=CPB, s=2, h=2)
        pt3 = pt[:, :].rearrange("p (c n) -> p c n", c=NCH)
        wo_hi = [cx_hi[:, s * W4:(s + 1) * W4] for s in range(2)]
        wo_lo = [cx_lo[:, s * W4:(s + 1) * W4] for s in range(2)]
        wq_hi = [v_hi[:, 0:W4], wv_hi[:, :]]
        wq_lo = [v_lo[:, 0:W4], wv_lo[:, :]]
        x_t = p_sb[0:TT, 0:NT * F].rearrange("p (t n) -> p t n", t=NT)
        XNW = F + 128
        xn_t = qo[0:TT, 0:NT * XNW].rearrange("p (t n) -> p t n", t=NT)
        xT = pt[:, 0:10 * TOK].rearrange("p (s f t) -> p s f t", s=2, f=NF + 1)
        ot_hi = [wk_hi[:, 0:HEADS4 * TOK], wv_hi[:, 0:HEADS4 * TOK]]
        ot_lo = [wk_lo[:, 0:HEADS4 * TOK], wv_lo[:, 0:HEADS4 * TOK]]
        w1h, w1l = cx_hi[:, 2 * W4:2 * W4 + HID], cx_lo[:, 2 * W4:2 * W4 + HID]
        w3h, w3l = v_hi[:, 0:HID], v_lo[:, 0:HID]
        w2h = v_hi[:, HID:HID + 3 * F].rearrange("p (j n) -> p j n", j=3)
        w2l = v_lo[:, HID:HID + 3 * F].rearrange("p (j n) -> p j n", j=3)
        o0 = NT * XNW
        b13_sb = qo[0:4, o0:o0 + 2 * HID].rearrange("p (s n) -> p s n", s=2)
        o0 += 2 * HID
        b2_sb = qo[0:2, o0:o0 + F]
        o0 += F
        t13 = qo[0:4, o0:o0 + TOK]
        o0 += TOK
        t2 = qo[0:2, o0:o0 + TOK]
        flat = stage[:, :, :].rearrange("p s n -> p (s n)")
        act_t = [flat[:, i * TOK:(i + 1) * TOK] for i in range(2)]
        asum = flat[:, 2 * TOK:5 * TOK].rearrange("p (j t) -> p j t", j=3)
        sig_t = [p_sb[:, NT * F + i * TOK:NT * F + (i + 1) * TOK] for i in range(2)]
        ash = k_hi[:, 0:3 * TOK].rearrange("p (j t) -> p j t", j=3)
        asl = k_lo[:, 0:3 * TOK].rearrange("p (j t) -> p j t", j=3)

        x_loaded = sem("x_loaded")
        small_loaded = sem("small_loaded")
        ident_zeroed = sem("ident_zeroed")
        ident_ready = sem("ident_ready")
        staged = [sem("staged0"), sem("staged1")]
        split_hi = sem("split_hi")
        split_done = sem("split_done")
        ln_step = sem("ln_step")
        var_ready = sem("var_ready")
        std_ready = sem("std_ready")
        xn_ready = sem("xn_ready")
        use_full = sem("use_full")
        use_hi = sem("use_hi")
        use_done = sem("use_done")
        q_spilled = [sem(f"q_spilled{j}") for j in range(4)]
        q_loaded = [sem(f"q_loaded{j}") for j in range(4)]
        qs_hi_ready = sem("qs_hi_ready")
        qs_ready = sem("qs_ready")
        score_full = sem("score_full")
        max_ready = sem("max_ready")
        exp_ready = sem("exp_ready")
        recip_ready = sem("recip_ready")
        prob_ready = sem("prob_ready")
        tr_full = sem("tr_full")
        tr_hi = sem("tr_hi")
        tr_done = sem("tr_done")
        o_spilled = [sem(f"o_spilled{j}") for j in range(4)]
        o_loaded = [sem(f"o_loaded{j}") for j in range(4)]
        ot_hi_ready = sem("ot_hi_ready")
        ot_ready = sem("ot_ready")
        blk_used = sem("blk_used")
        y_full = sem("y_full")
        gate_ready = sem("gate_ready")
        x1_ready = sem("x1_ready")
        bz_zeroed = sem("bz_zeroed")
        b_loaded = sem("b_loaded")
        a_hi = sem("a_hi")
        a_ready = sem("a_ready")
        t13_full = sem("t13_full")
        t13_ready = sem("t13_ready")
        h_full = sem("h_full")
        h_exp = sem("h_exp")
        ffn_step = sem("ffn_step")
        act_ready = sem("act_ready")
        t2_full = sem("t2_full")
        t2_ready = sem("t2_ready")
        as_hi = sem("as_hi")
        as_ready = sem("as_ready")
        y2_full = sem("y2_full")
        out_ready = sem("out_ready")
        out_stored = sem("out_stored")

        block = es.enter_context(nc.Block())

        def first_use(it):
            return it * BODY + (MAIN0 + QUARTERS)

        def head_cols(j):
            return slice(j * HEADS4 * TOK, (j + 1) * HEADS4 * TOK)

        def each_step(eng, body):
            for g in range(G):
                with eng.Fori(0, B - 1) as b:
                    body(b + g * B, g, b, NEXT_BATCH)
                body(g * B + B - 1, g, B - 1, NEXT_GROUP if g == 0 else LAST)

        @block.sync
        def _(sp):
            def load(slot, width, src):
                sp.dma_start(stage[:, slot, 0:width], src).then_inc(staged[slot], 16)

            sp.dma_start(x_t, x.rearrange("(t p) n -> p t n", p=TT)).then_inc(x_loaded, 16)
            def load_next(n, width, src):
                sp.wait_ge(split_done, n - 1)
                load(n % 2, width, src)

            def parts(l0, dl, turn_batch):
                for q in range(QUARTERS):
                    sp.wait_ge(split_done, dl + (l0 + q - 1))
                    load((l0 + q) % 2, NF * PW[q], part(turn_batch, q))

            load(0, W4, wq[4])
            load(1, W4, wq[5])
            sp.dma_start(gates[:, 0:1], gx.partition_broadcast(128)).then_inc(small_loaded, 16)
            sp.dma_start(gates[:, 1:2], gf.partition_broadcast(128)).then_inc(small_loaded, 16)
            sp.dma_start(a13_raw[:, :, :], a13).then_inc(small_loaded, 16)
            sp.dma_start(a2_sb[:, :, :], a2).then_inc(small_loaded, 16)
            for k in range(2, NG4):
                load_next(k, W4, wq[(k + 4) % NG4])
                if k < 6:
                    j = k - 2
                    sp.wait_ge(use_done, LN_USES + HEADS4 * (j + 1))
                    sp.dma_start(q_dram[:, head_cols(j)], qo[:, head_cols(j)]).then_inc(q_spilled[j], 16)
            load_next(L_WK, W4, wk[0])
            parts(L_CTX0, 0, ctx[0])
            load_next(L_WV, W4, wv[0])
            for g in range(G):
                with sp.Fori(0, B - 1) as b:
                    parts(L_LOOP[g], b * QUARTERS, ctx[b + 1])
                if g > 0:
                    break
                load_next(L_SWITCH, NF * PW[0], part(ctx[0], 0))
                load_next(L_SWITCH + 1, NF * PW[1], part(ctx[0], 1))

                def exchange(j):
                    sp.wait_ge(use_done, first_use(B - 1) + U_O[j] + 1)
                    sp.dma_start(o_dram[:, head_cols(j)], qo[:, head_cols(j)]).then_inc(o_spilled[j], 16)
                    sp.wait_ge(q_spilled[j], 16)
                    sp.wait_ge(o_spilled[j], 16)
                    sp.dma_start(qo[:, head_cols(j)], q_dram[:, head_cols(j)]).then_inc(q_loaded[j], 16)

                exchange(0)
                exchange(1)
                load_next(L_SWITCH + 2, NF * PW[2], part(ctx[0], 2))
                load_next(L_SWITCH + 3, W4, wk[1])
                load_next(L_SWITCH + 4, W4, wv[1])
                load_next(L_SWITCH + 5, NF * PW[3], part(ctx[0], 3))
                exchange(2)
                exchange(3)

            for k in range(NG4):
                load_next(L_WO + k, W4, wo[(k + 4) % NG4])
                if 2 <= k < 6:
                    sp.wait_ge(ot_ready, k - 1)
                    sp.dma_start(qo[:, head_cols(k - 2)], o_dram[:, head_cols(k - 2)]).then_inc(o_loaded[k - 2], 16)
            for i, (w, width) in enumerate(((w1, HID), (w3, HID), (w2, 3 * F))):
                load_next(L_FFN + i, width, w)
            sp.dma_start(x_t, x.rearrange("(t p) n -> p t n", p=TT)).then_inc(x_loaded, 16)
            sp.wait_ge(bz_zeroed, 1)
            sp.dma_start(b13_sb[0:2, 0, :], b13[0]).then_inc(b_loaded, 16)
            sp.dma_start(b13_sb[2:4, 1, :], b13[1]).then_inc(b_loaded, 16)
            sp.dma_start(b2_sb, b2).then_inc(b_loaded, 16)
            for t in range(NT):
                sp.wait_ge(out_ready, t + 1)
                sp.dma_start(out[t * TT:(t + 1) * TT, :], x_t[:, t, :]).then_inc(out_stored, 16)
            sp.wait_ge(out_stored, NT * 16)
            sp.wait_ge(small_loaded, 4 * 16)

        @block.gpsimd
        def _(pool):
            nc.gpsimd.memset(ident[:, :], 0.0).then_inc(ident_zeroed, 1)
            pool.wait_ge(ident_zeroed, 1)
            nc.gpsimd.affine_select(out=ident[:, :], in_=ident[:, :], compare_op=ALU.not_equal, fill=1.0,
                                    base=0, pattern=[[-1, 128]], channel_multiplier=1).then_inc(ident_ready, 1)

            def lo_part(n, slot, width, hi, lo):
                pool.wait_ge(split_hi, n + 1)
                nc.gpsimd.tensor_tensor(lo, stage[:, slot, 0:width], hi.bitcast(F32),
                                        ALU.subtract).then_inc(split_done, 1)

            def ctx_lo(n, slot, q):
                lo_part(n, slot, NF * PW[q], part(cx_hi, q), part(cx_lo, q))

            for k in range(NG4):
                lo_part(k, k % 2, W4, wq_hi[k % 2], wq_lo[k % 2])
            lo_part(L_WK, L_WK % 2, W4, wk_hi[:, :], wk_lo[:, :])
            for q in range(QUARTERS):
                ctx_lo(L_CTX0 + q, (L_CTX0 + q) % 2, q)
            lo_part(L_WV, L_WV % 2, W4, wv_hi[:, :], wv_lo[:, :])

            def body(it, g, b, then):
                if then == NEXT_BATCH:
                    for q in range(QUARTERS):
                        ctx_lo(b * QUARTERS + (L_LOOP[g] + q), q % 2, q)
                elif then == NEXT_GROUP:
                    for q in range(3):
                        ctx_lo(L_SWITCH + q, q % 2, q)
                    lo_part(L_SWITCH + 3, 1, W4, wk_hi[:, :], wk_lo[:, :])
                    lo_part(L_SWITCH + 4, 0, W4, wv_hi[:, :], wv_lo[:, :])
                    ctx_lo(L_SWITCH + 5, 1, 3)

            each_step(pool, body)
            for k in range(NG4):
                lo_part(L_WO + k, k % 2, W4, wo_hi[k % 2], wo_lo[k % 2])
            lo_part(L_FFN, 0, HID, w1h, w1l)
            lo_part(L_FFN + 1, 1, HID, w3h, w3l)
            lo_part(L_FFN + 2, 0, 3 * F, v_hi[:, HID:HID + 3 * F], v_lo[:, HID:HID + 3 * F])

        @block.scalar
        def _(act):
            copy = ACT.Copy

            def hi_part(l0, width, hi, later=0):
                slot = l0 % 2
                act.wait_ge(staged[slot], later * 16 + (l0 // 2 + 1) * 16)
                nc.scalar.activation(hi, stage[:, slot, 0:width], copy).then_inc(split_hi, 1)

            def take(n, dst, src):
                act.wait_ge(use_full, n + 1)
                nc.scalar.activation(dst, src, copy).then_inc(use_hi, 1)

            def layernorm_std(i):
                act.wait_ge(var_ready, i + 1)
                nc.scalar.activation(std[0:TT, :], std[0:TT, :], ACT.Sqrt).then_inc(std_ready, 1)

            layernorm_std(0)
            hi_part(0, W4, wq_hi[0])
            hi_part(1, W4, wq_hi[1])
            for f in range(NF):
                take(f, xT[:, 0, f, :], ring[f % 2][:, 0:TOK])
            for k in range(NG4):
                for j in range(HEADS4):
                    n = LN_USES + k * HEADS4 + j
                    if k >= 4 and j == 0:
                        act.wait_ge(q_spilled[k - 4], 16)
                    h = (k % 4) * HEADS4 + j
                    act.wait_ge(use_full, n + 1)
                    nc.scalar.activation(qo[:, h * TOK:(h + 1) * TOK], ring[n % 2][:, 0:TOK], copy,
                                         scale=SCALE).then_inc(use_done, 1)
                if k == NG4 - 2:
                    hi_part(L_WK, W4, wk_hi[:, :])
                    hi_part(L_CTX0, NF * PW[0], part(cx_hi, 0))
                if k == NG4 - 1:
                    for q in range(1, QUARTERS):
                        hi_part(L_CTX0 + q, NF * PW[q], part(cx_hi, q))
                    hi_part(L_WV, W4, wv_hi[:, :])
                if k + 2 < NG4:
                    hi_part(k + 2, W4, wq_hi[k % 2])

            def k_use(n, bank, q):
                take(n, k_hi[:, P0[q]:P0[q] + PW[q]], ring[bank][:, 0:PW[q]])

            def v_use(n, bank, c):
                take(n, vh[0:CH, c, :], ring[bank][0:CH, 0:VW])

            def o_use(n, bank):
                take(n, otmp[:, :], ring[bank][:, 2 * ROWS:4 * ROWS])

            def exp_half(step, h):
                act.wait_ge(max_ready, step * 2 + h + 1)
                nc.scalar.activation(ph[0:ROWS, h, :].rearrange("p (t n) -> p t n", t=THIRDS),
                                     banks[0:ROWS, 3 * h:3 * h + 3, 0:T3], ACT.Exp, bias=negmax[0:ROWS, h:h + 1],
                                     accum_out=psum_row[0:ROWS, h:h + 1]).then_inc(exp_ready, 1)

            def transposed(step):
                for j in range(NPT):
                    act.wait_ge(tr_full, step * NPT + j + 1)
                    for h in range(2):
                        ins = nc.scalar.activation(
                            pt6[0:CH, j, :, 0, h, :],
                            banks[0:CH, 3 * h + j, 0:CPB * ROWS].rearrange("p (c r) -> p c r", c=CPB), copy)
                    ins.then_inc(tr_hi, 1)

            def split_q(it, g, b, p):
                if g == 1:
                    act.wait_ge(q_loaded[p], 16)
                h = slice(p * REP, (p + 1) * REP)
                nc.scalar.activation(qsh3[:, h, :], qo3[:, h, bass.ts(b, TQ)], copy).then_inc(qs_hi_ready, 1)

            def split_out(k):
                nc.scalar.activation(ot_hi[k % 2], qo[:, head_cols(k % 4)], copy).then_inc(ot_hi_ready, 1)

            def body(it, g, b, then):
                u = first_use(it)
                step = it * PAIRS
                split_q(it, g, b, 0)
                for c in range(V_USES):
                    v_use(u + c, c % 2, c)
                for p in (0, 1):
                    k0 = U_K[p + 1]
                    exp_half(step + p, 0)
                    k_use(u + k0, k0 % 2, 0)
                    exp_half(step + p, 1)
                    k_use(u + k0 + 1, (k0 + 1) % 2, 1)
                    k_use(u + k0 + 2, k0 % 2, 2)
                    split_q(it, g, b, p + 1)
                    transposed(step + p)
                    k_use(u + k0 + 3, (k0 + 1) % 2, 3)
                    o_use(u + U_O[p], U_O[p] % 2)
                for q in range(QUARTERS):
                    n = U_KV + q + PC0[q]
                    if q == 0:
                        exp_half(step + 2, 0)
                    if q == 3:
                        split_q(it, g, b, 3)
                        transposed(step + 2)
                    k_use(u + n, n % 2, q)
                    if q == 0:
                        exp_half(step + 2, 1)
                    if q == 3 and then == NEXT_GROUP:
                        hi_part(L_SWITCH + 3, W4, wk_hi[:, :])
                    for c in range(PCH[q]):
                        v_use(u + n + 1 + c, (n + 1 + c) % 2, PC0[q] + c)
                    if then == NEXT_BATCH:
                        hi_part(L_LOOP[g] + q, NF * PW[q], part(cx_hi, q), later=b * 2)
                    elif then == NEXT_GROUP:
                        if q == 3:
                            hi_part(L_SWITCH + 4, W4, wv_hi[:, :])
                        hi_part(L_SWITCH + (q if q < 3 else 5), NF * PW[q], part(cx_hi, q))
                    elif q in (1, 3):
                        hi_part(L_WO + q // 2, W4, wo_hi[q // 2])
                exp_half(step + 3, 0)
                exp_half(step + 3, 1)
                o_use(u + U_O[2], U_O[2] % 2)
                if then == LAST:
                    transposed(step + 3)
                    split_out(0)
                    o_use(u + U_O[3] - QUARTERS, U_O[3] % 2)
                    return
                for q in range(3):
                    k_use(u + U_K0 + q, (U_K0 + q) % 2, q)
                transposed(step + 3)
                k_use(u + U_K0 + 3, (U_K0 + 3) % 2, 3)
                o_use(u + U_O[3], U_O[3] % 2)

            for q in range(QUARTERS):
                k_use(MAIN0 + q, q % 2, q)
            each_step(act, body)

            act.wait_ge(small_loaded, 4 * 16)
            nc.scalar.activation(tgate[:, :], gates[:, :], ACT.Tanh).then_inc(gate_ready, 1)
            nc.scalar.activation(a13_hi[:, :, :], a13_raw[:, :, :], copy).then_inc(a_hi, 1)
            for k in range(1, NG4):
                if k >= 2:
                    act.wait_ge(blk_used, k - 1)
                    hi_part(L_WO + k, W4, wo_hi[k % 2])
                if k == 3:
                    act.wait_ge(use_done, END)
                if k >= 4:
                    act.wait_ge(o_loaded[k - 4], 16)
                split_out(k)
            hi_part(L_FFN, HID, w1h)
            hi_part(L_FFN + 1, HID, w3h)
            hi_part(L_FFN + 2, 3 * F, v_hi[:, HID:HID + 3 * F])
            layernorm_std(1)
            for f in range(NF + 1):
                take(END + f, xT[:, 0, f, :], ring[f % 2][:, 0:TOK])
            act.wait_ge(t13_full, 1)
            nc.scalar.activation(t13, ring[1][0:4, 0:TOK], copy, scale=LORA).then_inc(t13_ready, 1)
            for c, (_, n, _) in enumerate(HCH):
                act.wait_ge(h_full, c + 1)
                if c >= 2:
                    act.wait_ge(act_ready, c - 1)
                nc.scalar.activation(sig_t[c % 2][0:n, :], banks[0:n, c % 2, 0:TOK], ACT.Exp,
                                     scale=-1.0).then_inc(h_exp, 1)
            act.wait_ge(t2_full, 1)
            nc.scalar.activation(t2, ring[0][0:2, 0:TOK], copy, scale=LORA).then_inc(t2_ready, 1)
            act.wait_ge(act_ready, len(HCH))
            for j, (_, n) in enumerate(HCUT):
                nc.scalar.activation(ash[0:n, j, :], asum[0:n, j, :], copy).then_inc(as_hi, 1)

        @block.vector
        def _(dve):
            def rest(n, dst, src, hi, skipped=Q_USES):
                dve.wait_ge(use_hi, n + 1 - skipped)
                nc.vector.tensor_tensor(dst, src, hi.bitcast(F32), ALU.subtract).then_inc(use_done, 1)

            def layernorm(i, xs):
                for t in range(NT):
                    nc.vector.bn_stats(stats[0:TT, t, :], x_t[:, t, :]).then_inc(ln_step, 1)
                for t in range(NT):
                    dve.wait_ge(ln_step, step_of[0] + t + 1)
                    nc.vector.bn_aggr(mv[0:TT, t, :], stats[0:TT, t, :]).then_inc(ln_step, 1)
                dve.wait_ge(ln_step, step_of[0] + 2 * NT)
                nc.vector.tensor_scalar(std[0:TT, :], mv[0:TT, :, 1], EPS, None, ALU.add).then_inc(var_ready, 1)
                dve.wait_ge(std_ready, i + 1)
                nc.vector.reciprocal(rstd[0:TT, :], std[0:TT, :]).then_inc(ln_step, 1)
                dve.wait_ge(ln_step, step_of[0] + 2 * NT + 1)
                for t in range(NT):
                    ins = nc.vector.tensor_scalar(xn_t[:, t, 0:F], x_t[:, t, :], mv[0:TT, t, 0:1], rstd[0:TT, t:t + 1],
                                                  ALU.subtract, ALU.mult)
                    if not xs:
                        ins.then_inc(xn_ready, 1)
                        continue
                    ins.then_inc(ln_step, 1)
                step_of[0] += 2 * NT + 1

            step_of = [0]
            dve.wait_ge(x_loaded, 16)
            layernorm(0, False)
            for f in range(NF):
                rest(f, xT[:, 1, f, :], ring[f % 2][:, 0:TOK], xT[:, 0, f, :], skipped=0)
            def k_use(n, bank, q):
                c = slice(P0[q], P0[q] + PW[q])
                rest(n, k_lo[:, c], ring[bank][:, 0:PW[q]], k_hi[:, c])

            def v_use(n, bank, c):
                rest(n, vl[0:CH, c, :], ring[bank][0:CH, 0:VW], vh[0:CH, c, :])

            def o_use(n, bank, b, p, skipped=Q_USES):
                dve.wait_ge(use_hi, n + 1 - skipped)
                nc.vector.tensor_tensor(qo3[:, p * REP:(p + 1) * REP, bass.ts(b, TQ)],
                                        ring[bank][:, 0:2 * ROWS].rearrange("p (h t) -> p h t", h=REP),
                                        otmp[:, :].rearrange("p (h t) -> p h t", h=REP),
                                        ALU.add).then_inc(use_done, 1)

            def max_half(step, h):
                dve.wait_ge(score_full, step * 2 + h + 1)
                nc.vector.tensor_reduce(negmax[0:ROWS, h:h + 1], banks[0:ROWS, 3 * h:3 * h + 3, 0:T3], AX.XY,
                                        ALU.max, negate=True).then_inc(max_ready, 1)

            def normalise(step, h):
                n = step * 2 + h + 1
                dve.wait_ge(exp_ready, n)
                nc.vector.reciprocal(rinv[0:ROWS, h:h + 1], psum_row[0:ROWS, h:h + 1]).then_inc(recip_ready, 1)
                dve.wait_ge(recip_ready, n)
                nc.vector.tensor_scalar(ph[0:ROWS, h, :], ph[0:ROWS, h, :], rinv[0:ROWS, h:h + 1], None,
                                        ALU.mult).then_inc(prob_ready, 1)

            def transposed(step):
                for j in range(NPT):
                    dve.wait_ge(tr_hi, step * NPT + j + 1)
                    for h in range(2):
                        ins = nc.vector.tensor_tensor(
                            pt6[0:CH, j, :, 1, h, :],
                            banks[0:CH, 3 * h + j, 0:CPB * ROWS].rearrange("p (c r) -> p c r", c=CPB),
                            pt6[0:CH, j, :, 0, h, :].bitcast(F32), ALU.subtract)
                    ins.then_inc(tr_done, 1)

            def split_q(it, b, p):
                dve.wait_ge(qs_hi_ready, it * PAIRS + (p + 1))
                h = slice(p * REP, (p + 1) * REP)
                nc.vector.tensor_tensor(qsl3[:, h, :], qo3[:, h, bass.ts(b, TQ)], qsh3[:, h, :].bitcast(F32),
                                        ALU.subtract).then_inc(qs_ready, 1)

            def split_out(k):
                dve.wait_ge(ot_hi_ready, k + 1)
                nc.vector.tensor_tensor(ot_lo[k % 2], qo[:, head_cols(k % 4)], ot_hi[k % 2].bitcast(F32),
                                        ALU.subtract).then_inc(ot_ready, 1)

            def body(it, g, b, then):
                u = first_use(it)
                step = it * PAIRS
                split_q(it, b, 0)
                for c in range(V_USES):
                    v_use(u + c, c % 2, c)
                for p in (0, 1):
                    k0 = U_K[p + 1]
                    max_half(step + p, 0)
                    max_half(step + p, 1)
                    normalise(step + p, 0)
                    k_use(u + k0, k0 % 2, 0)
                    normalise(step + p, 1)
                    k_use(u + k0 + 1, (k0 + 1) % 2, 1)
                    k_use(u + k0 + 2, k0 % 2, 2)
                    split_q(it, b, p + 1)
                    transposed(step + p)
                    k_use(u + k0 + 3, (k0 + 1) % 2, 3)
                    o_use(u + U_O[p], U_O[p] % 2, b, p)
                max_half(step + 2, 0)
                max_half(step + 2, 1)
                for q in range(QUARTERS):
                    n = U_KV + q + PC0[q]
                    if q == 0:
                        normalise(step + 2, 0)
                    if q == 3:
                        split_q(it, b, 3)
                        transposed(step + 2)
                    k_use(u + n, n % 2, q)
                    if q == 0:
                        normalise(step + 2, 1)
                    for c in range(PCH[q]):
                        v_use(u + n + 1 + c, (n + 1 + c) % 2, PC0[q] + c)
                max_half(step + 3, 0)
                max_half(step + 3, 1)
                normalise(step + 3, 0)
                normalise(step + 3, 1)
                o_use(u + U_O[2], U_O[2] % 2, b, 2)
                if then == LAST:
                    transposed(step + 3)
                    split_out(0)
                    o_use(u + U_O[3] - QUARTERS, U_O[3] % 2, b, 3)
                    return
                for q in range(3):
                    k_use(u + U_K0 + q, (U_K0 + q) % 2, q)
                transposed(step + 3)
                k_use(u + U_K0 + 3, (U_K0 + 3) % 2, 3)
                o_use(u + U_O[3], U_O[3] % 2, b, 3)

            for q in range(QUARTERS):
                k_use(MAIN0 + q, q % 2, q)
            each_step(dve, body)

            dve.wait_ge(a_hi, 1)
            nc.vector.tensor_tensor(a13_lo[:, :, :], a13_raw[:, :, :], a13_hi[:, :, :].bitcast(F32),
                                    ALU.subtract).then_inc(a_ready, 1)
            for k in range(1, NG4):
                split_out(k)
            dve.wait_ge(ot_ready, NG4)
            nc.vector.memset(b13_sb, 0.0).then_inc(bz_zeroed, 1)
            dve.wait_ge(gate_ready, 1)
            dve.wait_ge(x_loaded, 2 * 16)
            for t in range(NT):
                dve.wait_ge(y_full, t + 1)
                nc.vector.scalar_tensor_tensor(x_t[:, t, :], banks[0:TT, t, :], tgate[0:TT, 0:1], x_t[:, t, :],
                                               ALU.mult, ALU.add).then_inc(x1_ready, 1)
            dve.wait_ge(x1_ready, NT)
            layernorm(1, True)
            dve.wait_ge(ln_step, step_of[0] + NT)
            for t in range(NT):
                nc.vector.tensor_reduce(xn_t[:, t, F:F + 128], xn_t[:, t, 0:F].rearrange("p (f n) -> p n f", f=NF),
                                        AX.X, ALU.add).then_inc(xn_ready, 1)
            for f in range(NF + 1):
                rest(END + f, xT[:, 1, f, :], ring[f % 2][:, 0:TOK], xT[:, 0, f, :])
            step = 0
            dve.wait_ge(split_done, L_FFN + 3)
            for c, (_, n, j) in enumerate(HCH):
                sg = sig_t[c % 2][0:n, :]
                ac = act_t[c % 2][0:n, :]
                dve.wait_ge(h_exp, c + 1)
                nc.vector.tensor_scalar(sg, sg, 1.0, None, ALU.add).then_inc(ffn_step, 1)
                dve.wait_ge(ffn_step, step + 1)
                nc.vector.reciprocal(sg, sg).then_inc(ffn_step, 1)
                dve.wait_ge(ffn_step, step + 2)
                nc.vector.tensor_tensor(sg, banks[0:n, c % 2, 0:TOK], sg, ALU.mult).then_inc(ffn_step, 1)
                dve.wait_ge(ffn_step, step + 3)
                nc.vector.tensor_tensor(ac, banks[0:n, 2 + c % 2, 0:TOK], sg, ALU.mult).then_inc(ffn_step, 1)
                dve.wait_ge(ffn_step, step + 4)
                step += 4
                if c < 3:
                    nc.vector.tensor_copy(asum[0:n, j, :], ac).then_inc(act_ready, 1)
                else:
                    nc.vector.tensor_tensor(asum[0:n, j, :], asum[0:n, j, :], ac, ALU.add).then_inc(act_ready, 1)
            for j, (_, n) in enumerate(HCUT):
                dve.wait_ge(as_hi, j + 1)
                nc.vector.tensor_tensor(asl[0:n, j, :], asum[0:n, j, :], ash[0:n, j, :].bitcast(F32),
                                        ALU.subtract).then_inc(as_ready, 1)
            for t in range(NT):
                dve.wait_ge(y2_full, t + 1)
                nc.vector.scalar_tensor_tensor(x_t[:, t, :], banks[0:TT, t, :], tgate[0:TT, 1:2], x_t[:, t, :],
                                               ALU.mult, ALU.add).then_inc(out_ready, 1)

        @block.tensor
        def _(pe):
            def three(dst, ah, al, bh, bl, first, last):
                nc.tensor.matmul(dst, ah, bh, start=first, stop=False)
                nc.tensor.matmul(dst, ah, bl, start=False, stop=False)
                return nc.tensor.matmul(dst, al, bh, start=False, stop=last)

            def bank_free(n):
                pe.wait_ge(use_done, n - 1)

            def transposes(n0, nf):
                for f in range(nf):
                    if n0 + f >= 2:
                        bank_free(n0 + f)
                    for t in range(NT):
                        ins = nc.tensor.transpose(ring[f % 2][:, t * TT:(t + 1) * TT],
                                                  xn_t[:, t, f * 128:(f + 1) * 128], ident[0:TT, 0:TT])
                    ins.then_inc(use_full, 1)

            pe.wait_ge(ident_ready, 1)
            pe.wait_ge(xn_ready, NT)
            transposes(0, NF)
            pe.wait_ge(use_done, LN_USES)
            for k in range(NG4):
                pe.wait_ge(split_done, k + 1)
                wh, wl = w4(wq_hi[k % 2]), w4(wq_lo[k % 2])
                for j in range(HEADS4):
                    n = LN_USES + k * HEADS4 + j
                    bank_free(n)
                    for f in range(NF):
                        ins = three(ring[n % 2][:, 0:TOK], wh[:, f, j * D:(j + 1) * D], wl[:, f, j * D:(j + 1) * D],
                                    xT[:, 0, f, :], xT[:, 1, f, :], f == 0, f == NF - 1)
                    ins.then_inc(use_full, 1)

            def k_use(n, bank, p, q):
                bank_free(n)
                c = slice(p * D, (p + 1) * D)
                for f in range(NF):
                    ins = three(ring[bank][:, 0:PW[q]], wkh[:, f, c], wkl[:, f, c], cxh[q][:, f, :], cxl[q][:, f, :],
                                f == 0, f == NF - 1)
                ins.then_inc(use_full, 1)

            def v_use(n, bank, s, c):
                bank_free(n)
                q = max(i for i in range(QUARTERS) if PC0[i] <= c)
                i = slice((c - PC0[q]) * CH, (c - PC0[q] + 1) * CH)
                for f in range(NF):
                    ins = three(ring[bank][0:CH, 0:VW], cxh[q][:, f, i], cxl[q][:, f, i],
                                wvh[:, f, s * VW:(s + 1) * VW], wvl[:, f, s * VW:(s + 1) * VW], f == 0, f == NF - 1)
                ins.then_inc(use_full, 1)

            def scores(p, keys_done):
                pe.wait_ge(use_done, keys_done)
                for h in range(2):
                    r = slice((p * REP + 2 * h) * TQ, (p * REP + 2 * h) * TQ + ROWS)
                    for t in range(THIRDS):
                        c = slice(t * T3, (t + 1) * T3)
                        ins = three(banks[0:ROWS, 3 * h + t, 0:T3], qs_hi[:, r], qs_lo[:, r], k_hi[:, c], k_lo[:, c],
                                    True, True)
                    ins.then_inc(score_full, 1)

            def transpose_probs(step):
                for j in range(NPT):
                    for h in range(2):
                        if j == 0:
                            pe.wait_ge(prob_ready, step * 2 + h + 1)
                        for c in range(CPB):
                            at = (j * CPB + c) * CH
                            ins = nc.tensor.transpose(banks[0:CH, 3 * h + j, c * ROWS:(c + 1) * ROWS],
                                                      ph[0:ROWS, h, at:at + CH], ident[0:ROWS, 0:ROWS])
                    ins.then_inc(tr_full, 1)

            def weigh(n, bank, step, p):
                bank_free(n)
                i = slice(p % 2 * D, (p % 2 + 1) * D)
                for c in range(NCH):
                    if c % CPB == 0:
                        pe.wait_ge(tr_done, step * NPT + c // CPB + 1)
                    if c > 0:
                        nc.tensor.matmul(ring[bank][:, 0:2 * ROWS], vl[0:CH, c, i], pt3[0:CH, c, 0:2 * ROWS],
                                         start=False, stop=False)
                    ins = nc.tensor.matmul(ring[bank][:, 0:4 * ROWS], vh[0:CH, c, i], pt3[0:CH, c, :],
                                           start=(c == 0), stop=(c == NCH - 1))
                    if c == 0:
                        nc.tensor.matmul(ring[bank][:, 0:2 * ROWS], vl[0:CH, c, i], pt3[0:CH, c, 0:2 * ROWS],
                                         start=False, stop=False)
                ins.then_inc(use_full, 1)

            def body(it, g, b, then):
                u = first_use(it)
                step = it * PAIRS
                for c in range(V_USES):
                    v_use(u + c, c % 2, 0, c)
                for p in (0, 1):
                    k0 = U_K[p + 1]
                    pe.wait_ge(qs_ready, step + (p + 1))
                    scores(p, u - 1 if p == 0 else u + U_O[p - 1])
                    for q in range(3):
                        k_use(u + k0 + q, (k0 + q) % 2, p + 1, q)
                    transpose_probs(step + p)
                    k_use(u + k0 + 3, (k0 + 3) % 2, p + 1, 3)
                    weigh(u + U_O[p], U_O[p] % 2, step + p, p)
                pe.wait_ge(qs_ready, step + 3)
                scores(2, u + U_O[1])
                for q in range(QUARTERS):
                    n = U_KV + q + PC0[q]
                    if q == 3:
                        transpose_probs(step + 2)
                    k_use(u + n, n % 2, 3, q)
                    for c in range(PCH[q]):
                        v_use(u + n + 1 + c, (n + 1 + c) % 2, 1, PC0[q] + c)
                pe.wait_ge(tr_done, (step + 3) * NPT)
                pe.wait_ge(qs_ready, step + 4)
                scores(3, u + U_KV + 3 + PC0[3] + 1)
                pe.wait_ge(use_done, u + U_O[2])
                weigh(u + U_O[2], U_O[2] % 2, step + 2, 2)
                if then == LAST:
                    transpose_probs(step + 3)
                    weigh(u + U_O[3] - QUARTERS, U_O[3] % 2, step + 3, 3)
                    return
                for q in range(QUARTERS):
                    if q == 3:
                        transpose_probs(step + 3)
                    if then == NEXT_BATCH:
                        pe.wait_ge(split_done, b * QUARTERS + (L_LOOP[g] + q + 1))
                    else:
                        pe.wait_ge(split_done, L_SWITCH + 3 + 1 if q < 3 else L_SWITCH + 5 + 1)
                    k_use(u + U_K0 + q, (U_K0 + q) % 2, 0, q)
                weigh(u + U_O[3], U_O[3] % 2, step + 3, 3)

            for q in range(QUARTERS):
                pe.wait_ge(split_done, L_CTX0 + q + 1)
                k_use(MAIN0 + q, q % 2, 0, q)
            pe.wait_ge(split_done, L_WV + 1)
            each_step(pe, body)

            pe.wait_ge(tr_done, G * B * PAIRS * NPT)
            for k in range(NG4):
                pe.wait_ge(split_done, L_WO + k + 1)
                pe.wait_ge(ot_ready, k + 1)
                wh, wl = w4(wo_hi[k % 2]), w4(wo_lo[k % 2])
                order = [(j, t) for j in range(HEADS4) for t in range(NT)]
                if k == NG4 - 1:
                    order = [(j, t) for t in range(NT) for j in range(HEADS4)]
                for j, t in order:
                    c = slice(j * TOK + t * TT, j * TOK + (t + 1) * TT)
                    first, last = k == 0 and j == 0, k == NG4 - 1 and j == HEADS4 - 1
                    ins = three(banks[0:TT, t, :], ot_hi[k % 2][:, c], ot_lo[k % 2][:, c], wh[:, j, :], wl[:, j, :],
                                first, last)
                    if last:
                        ins.then_inc(y_full, 1)
                if k < NG4 - 1:
                    ins.then_inc(blk_used, 1)
            pe.wait_ge(xn_ready, 2 * NT)
            transposes(END, NF + 1)
            pe.wait_ge(a_ready, 1)
            pe.wait_ge(use_done, END + NF + 1)
            for f in range(NF):
                ins = three(ring[1][0:4, 0:TOK], a13_hi[:, f, :], a13_lo[:, f, :], xT[:, 0, f, :], xT[:, 1, f, :],
                            f == 0, f == NF - 1)
            ins.then_inc(t13_full, 1)
            pe.wait_ge(split_done, L_FFN + 3)
            pe.wait_ge(small_loaded, 4 * 16)
            pe.wait_ge(b_loaded, 3 * 16)
            pe.wait_ge(t13_ready, 1)

            def lora_down(c):
                n = HCH[c][1]
                pe.wait_ge(act_ready, c + 1)
                return nc.tensor.matmul(ring[0][0:2, 0:TOK], a2_sb[0:n, c, :], act_t[c % 2][0:n, :],
                                        start=(c == 0), stop=(c == len(HCH) - 1))

            for c, (at, n, _) in enumerate(HCH):
                if c >= 2:
                    lora_down(c - 2)
                hid = slice(at, at + n)
                for i, (wh, wl) in enumerate(((w1h, w1l), (w3h, w3l))):
                    dst = banks[0:n, 2 * i + c % 2, 0:TOK]
                    three(dst, wh[:, hid], wl[:, hid], xT[:, 0, NF, :], xT[:, 1, NF, :], True, False)
                    ins = nc.tensor.matmul(dst, b13_sb[:, i, hid], t13, start=False, stop=True)
                ins.then_inc(h_full, 1)
            lora_down(len(HCH) - 2)
            lora_down(len(HCH) - 1).then_inc(t2_full, 1)
            pe.wait_ge(t2_ready, 1)
            pe.wait_ge(as_ready, 3)
            for t in range(NT):
                c = slice(t * TT, (t + 1) * TT)
                for j, (_, n) in enumerate(HCUT):
                    three(banks[0:TT, t, :], ash[0:n, j, c], asl[0:n, j, c], w2h[0:n, j, :], w2l[0:n, j, :],
                          j == 0, False)
                nc.tensor.matmul(banks[0:TT, t, :], t2[:, c], b2_sb, start=False, stop=True).then_inc(y2_full, 1)


def kernel(x, ctx_4096, g_xattn, g_ffn, L0_xattn_wq, L0_xattn_wk, L0_xattn_wv, L0_xattn_wo, L0_ffn_w1q,
           L0_ffn_a1, L0_ffn_b1, L0_ffn_w3q, L0_ffn_a3, L0_ffn_b3, L0_ffn_w2q, L0_ffn_a2, L0_ffn_b2):
    import numpy as np
    import concourse.bacc as bacc
    from concourse.bass_utils import run_bass_kernel_spmd as run

    c = np.ascontiguousarray

    def blocks(w, n):
        w = np.asarray(w)
        return c(w.reshape(NF, 128, n, -1).transpose(2, 1, 0, 3).reshape(n, 128, -1))

    ctx = np.asarray(ctx_4096).reshape(B, TK, NF, 128).transpose(0, 3, 2, 1)
    ctx = np.concatenate([ctx[..., P0[q]:P0[q] + PW[q]].reshape(B, 128, -1) for q in range(QUARTERS)], -1)
    w2t = np.zeros((3 * 128, F), np.float32)
    w2t[:HQR] = np.asarray(L0_ffn_w2q).T
    a2t = np.zeros((128, len(HCH), 2), np.float32)
    for i, (at, n, _) in enumerate(HCH):
        a2t[:n, i] = np.asarray(L0_ffn_a2)[:, at:at + n].T
    a13 = np.concatenate([np.asarray(L0_ffn_a1), np.asarray(L0_ffn_a3)], 0)
    arrays = {
        "x": c(np.asarray(x).reshape(TOK, F)),
        "ctx": c(ctx),
        "gx": c(np.asarray(g_xattn)[:1]),
        "gf": c(np.asarray(g_ffn)[:1]),
        "wq": blocks(L0_xattn_wq, NG4),
        "wk": blocks(L0_xattn_wk, G),
        "wv": blocks(L0_xattn_wv, G),
        "wo": c(np.asarray(L0_xattn_wo).reshape(NG4, HEADS4, D, F).transpose(0, 2, 1, 3).reshape(NG4, 128, -1)),
        "w1": c(np.asarray(L0_ffn_w1q).T),
        "w3": c(np.asarray(L0_ffn_w3q).T),
        "w2": c(w2t.reshape(3, 128, F).transpose(1, 0, 2).reshape(128, 3 * F)),
        "a13": c(a13.T.reshape(NF, 128, 4).transpose(1, 0, 2)),
        "a2": a2t,
        "b13": c(np.stack([np.asarray(L0_ffn_b1).T, np.asarray(L0_ffn_b3).T])),
        "b2": c(np.asarray(L0_ffn_b2).T),
    }
    nc = bacc.Bacc("TRN2", target_bir_lowering=False, num_devices=1)
    args = [nc.dram_tensor(n, a.shape, mybir.dt.from_np(a.dtype), kind="ExternalInput").ap() for n, a in arrays.items()]
    out = nc.dram_tensor("out", (TOK, F), F32, kind="ExternalOutput").ap()
    q_dram = nc.dram_tensor("q_dram", (128, GH * TOK), F32).ap()
    o_dram = nc.dram_tensor("o_dram", (128, GH * TOK), F32).ap()
    flamingo_kernel(nc, *args, out, q_dram, o_dram)
    r = run(nc, [arrays], core_ids=[0])
    return r.results[0]["out"].reshape(B, TQ, F)
```

```python
from contextlib import ExitStack

import concourse.bass as bass
from concourse import mybir

F32 = mybir.dt.float32
F32R = mybir.dt.float32r
ALU = mybir.AluOpType
ACT = mybir.ActivationFunctionType
AX = mybir.AxisListType

B, TQ, F = 8, 56, 512
TK = 1500
HQ, HKV, D = 32, 8, 128
REP = HQ // HKV
HID = 1376
EPS = 1e-5
SCALE = 1.0 / float(D) ** 0.5
LORA = 0.5

NF = F // 128
TOK = B * TQ
TT = 112
NT = TOK // TT
G = 2
PAIRS = HKV // G
GH = HQ // G
QUARTERS = 4
CH = 125
NCH = TK // CH
PCH = (2, 4, 2, 4)
PC0 = tuple(sum(PCH[:q]) for q in range(QUARTERS))
PW = tuple(n * CH for n in PCH)
P0 = tuple(n * CH for n in PC0)
THIRDS = 3
T3 = TK // THIRDS
ROWS = 2 * TQ
CPB = 4
NPT = NCH // CPB
TR = [(h, j) for h in range(2) for j in range(NPT)]
VW = 2 * D
HEADS4 = 4
NG4 = HQ // HEADS4
W4 = NF * HEADS4 * D

HQR = HID // 4
HCUT = [(0, 128), (128, 128), (256, HQR - 256)]
HCH = [(q * HQR + o, n, j) for q in range(4) for j, (o, n) in enumerate(HCUT)]

LN_USES = NF
Q_USES = HQ
V_USES = NCH
BODY = 2 * V_USES + PAIRS * (QUARTERS + 1)
MAIN0 = LN_USES + Q_USES
END = MAIN0 + G * B * BODY
U_K = {1: V_USES, 2: V_USES + 5, 3: V_USES + 10}
U_O = {0: V_USES + 4, 1: V_USES + 9, 2: 2 * V_USES + 14, 3: 2 * V_USES + 19}
U_V23 = V_USES + 14
U_K0 = U_O[2] + 1
V_BANKS = (6, 3, 7, 4)

LN_BANKS = (6, 4, 5, 0, 7)
LN2_ORDER = (NF, *range(NF))
H_BANKS = ((1, 2), (3, 0), (4, 5))
T13_BANK, T2_BANK = 7, 6

FIRST = ("q0", "q1", "q2", "q3", "k", "q4", "c0", "q5", "c1", "q6", "c2", "q7", "c3", "v")
L_WQ = [FIRST.index(f"q{k}") for k in range(NG4)]
L_WK = FIRST.index("k")
L_CTX0 = [FIRST.index(f"c{q}") for q in range(QUARTERS)]
L_WV = FIRST.index("v")
L_LOOP = [L_WV + 1]
L_SWITCH = L_LOOP[0] + (B - 1) * QUARTERS
L_LOOP.append(L_SWITCH + QUARTERS + 2)
L_WO = L_LOOP[1] + (B - 1) * QUARTERS
L_FFN = L_WO + NG4
NEXT_BATCH, NEXT_GROUP, LAST = range(3)


def flamingo_kernel(nc, x, ctx, gx, gf, wq, wk, wv, wo, w1, w3, w2, a13, a2, b13, b2, out, q_dram, o_dram):
    es = ExitStack()
    with es:
        def sb(name, shape, dt=F32):
            return es.enter_context(nc.sbuf_tensor(name, shape, dt))

        def sem(name):
            return es.enter_context(nc.semaphore(name))

        stage = sb("stage", [128, 2, W4])
        wk_hi = sb("wk_hi", [128, W4], F32R)
        wk_lo = sb("wk_lo", [128, W4], F32R)
        wv_hi = sb("wv_hi", [128, W4], F32R)
        wv_lo = sb("wv_lo", [128, W4], F32R)
        cx_hi = sb("cx_hi", [128, NF * TK], F32R)
        cx_lo = sb("cx_lo", [128, NF * TK], F32R)
        v_hi = sb("v_hi", [128, NCH * VW], F32R)
        v_lo = sb("v_lo", [128, NCH * VW], F32R)
        k_hi = sb("k_hi", [128, TK], F32R)
        k_lo = sb("k_lo", [128, TK], F32R)
        qo = sb("qo", [128, GH * TOK])
        qs_hi = sb("qs_hi", [128, GH * TQ], F32R)
        qs_lo = sb("qs_lo", [128, GH * TQ], F32R)
        p_sb = sb("p_sb", [128, 2 * TK])
        pt = sb("pt", [128, NPT * CPB * 4 * ROWS], F32R)
        otmp = sb("otmp", [128, 2 * ROWS])
        ident = sb("ident", [128, 128])
        negmax = sb("negmax", [128, 2])
        row_sum = sb("row_sum", [128, 2])
        rinv = sb("rinv", [128, 2])
        stats = sb("stats", [128, NT, 6])
        mv = sb("mv", [128, NT, 2])
        std = sb("std", [128, NT])
        rstd = sb("rstd", [128, NT])
        gates = sb("gates", [128, 2])
        tgate = sb("tgate", [128, 2])
        a13_raw = sb("a13_raw", [128, NF, 4])
        a13_hi = sb("a13_hi", [128, NF, 4], F32R)
        a13_lo = sb("a13_lo", [128, NF, 4], F32R)

        banks = es.enter_context(nc.psum_tensor("banks", [128, 8, 512], F32))
        ring = [banks[:, 6, :], banks[:, 7, :]]

        def w4(t):
            return t[:, 0:W4].rearrange("p (f n) -> p f n", f=NF)
        wkh, wkl, wvh, wvl = w4(wk_hi), w4(wk_lo), w4(wv_hi), w4(wv_lo)

        def part(t, q):
            return t[:, NF * P0[q]:NF * (P0[q] + PW[q])]

        cxh = [part(cx_hi, q).rearrange("p (f t) -> p f t", f=NF) for q in range(QUARTERS)]
        cxl = [part(cx_lo, q).rearrange("p (f t) -> p f t", f=NF) for q in range(QUARTERS)]
        vh = v_hi[:, :].rearrange("p (c n) -> p c n", c=NCH)
        vl = v_lo[:, :].rearrange("p (c n) -> p c n", c=NCH)
        qo3 = qo[:, :].rearrange("p (h t) -> p h t", h=GH)
        qsh3 = qs_hi[:, :].rearrange("p (h t) -> p h t", h=GH)
        qsl3 = qs_lo[:, :].rearrange("p (h t) -> p h t", h=GH)
        ph = p_sb[:, :].rearrange("p (h t) -> p h t", h=2)
        pt6 = pt[:, :].rearrange("p (g c s h r) -> p g c s h r", g=NPT, c=CPB, s=2, h=2)
        pt3 = pt[:, :].rearrange("p (c n) -> p c n", c=NCH)
        wo_hi = [cx_hi[:, s * W4:(s + 1) * W4] for s in range(2)]
        wo_lo = [cx_lo[:, s * W4:(s + 1) * W4] for s in range(2)]
        wq_hi = [v_hi[:, 0:W4], wv_hi[:, :]]
        wq_lo = [v_lo[:, 0:W4], wv_lo[:, :]]
        x_t = p_sb[0:TT, 0:NT * F].rearrange("p (t n) -> p t n", t=NT)
        XNW = F + 128
        xn_t = qo[0:TT, 0:NT * XNW].rearrange("p (t n) -> p t n", t=NT)
        xT = pt[:, 0:10 * TOK].rearrange("p (s f t) -> p s f t", s=2, f=NF + 1)
        ot_hi = [wk_hi[:, 0:HEADS4 * TOK], wv_hi[:, 0:HEADS4 * TOK]]
        ot_lo = [wk_lo[:, 0:HEADS4 * TOK], wv_lo[:, 0:HEADS4 * TOK]]
        w1h, w1l = cx_hi[:, 2 * W4:2 * W4 + HID], cx_lo[:, 2 * W4:2 * W4 + HID]
        w3h, w3l = v_hi[:, 0:HID], v_lo[:, 0:HID]
        b1h, b1l = k_hi[0:4, 0:HID], k_lo[0:4, 0:HID]
        b3h, b3l = v_hi[0:4, HID:2 * HID], v_lo[0:4, HID:2 * HID]
        a2h, a2l = (t[:, 2 * HID:2 * HID + 2 * len(HCH)] for t in (v_hi, v_lo))
        w2h = wk_hi[:, 0:3 * F].rearrange("p (j n) -> p j n", j=3)
        w2l = wk_lo[:, 0:3 * F].rearrange("p (j n) -> p j n", j=3)
        t2h, t2l = wk_hi[0:2, 3 * F:3 * F + TOK], wk_lo[0:2, 3 * F:3 * F + TOK]
        ash = wv_hi[:, 0:3 * TOK].rearrange("p (j t) -> p j t", j=3)
        asl = wv_lo[:, 0:3 * TOK].rearrange("p (j t) -> p j t", j=3)
        b2h, b2l = wv_hi[0:2, 3 * TOK:3 * TOK + F], wv_lo[0:2, 3 * TOK:3 * TOK + F]
        t13h, t13l = pt[0:4, 10 * TOK:11 * TOK], pt[0:4, 11 * TOK:12 * TOK]
        o0 = NT * XNW
        act_t = [qo[:, o0 + i * TOK:o0 + (i + 1) * TOK] for i in range(2)]
        asum = qo[:, o0 + 2 * TOK:o0 + 5 * TOK].rearrange("p (j t) -> p j t", j=3)
        th_t = [p_sb[:, NT * F + i * TOK:NT * F + (i + 1) * TOK] for i in range(2)]
        acth = [qs_hi[:, i * TOK:(i + 1) * TOK] for i in range(2)]
        actl = [qs_lo[:, i * TOK:(i + 1) * TOK] for i in range(2)]

        x_loaded = [sem(f"x_loaded{t}") for t in range(NT)]
        small_loaded = sem("small_loaded")
        ident_zeroed = sem("ident_zeroed")
        ident_ready = sem("ident_ready")
        staged = [sem("staged0"), sem("staged1")]
        split_hi = sem("split_hi")
        split_done = sem("split_done")
        ln_step = sem("ln_step")
        var_ready = sem("var_ready")
        std_ready = sem("std_ready")
        xn_ready = sem("xn_ready")
        use_full = sem("use_full")
        use_hi = sem("use_hi")
        use_done = sem("use_done")
        q_spilled = [sem(f"q_spilled{j}") for j in range(4)]
        q_loaded = [sem(f"q_loaded{j}") for j in range(4)]
        qs_hi_ready = sem("qs_hi_ready")
        qs_ready = sem("qs_ready")
        score_full = sem("score_full")
        max_ready = sem("max_ready")
        exp_ready = sem("exp_ready")
        recip_ready = sem("recip_ready")
        prob_ready = sem("prob_ready")
        tr_full = sem("tr_full")
        tr_hi = sem("tr_hi")
        tr_done = sem("tr_done")
        o_spilled = [sem(f"o_spilled{j}") for j in range(4)]
        o_loaded = [sem(f"o_loaded{j}") for j in range(4)]
        ot_hi_ready = sem("ot_hi_ready")
        ot_ready = sem("ot_ready")
        blk_used = sem("blk_used")
        y_full = sem("y_full")
        gate_ready = sem("gate_ready")
        x1_ready = sem("x1_ready")
        a_hi = sem("a_hi")
        a_ready = sem("a_ready")
        t13_full = sem("t13_full")
        t13_hi = sem("t13_hi")
        t13_ready = sem("t13_ready")
        h_full = sem("h_full")
        h_tanh = sem("h_tanh")
        ffn_step = sem("ffn_step")
        act_ready = sem("act_ready")
        act_hi = sem("act_hi")
        act_split = sem("act_split")
        act_summed = sem("act_summed")
        down_done = sem("down_done")
        t2_hi = sem("t2_hi")
        t2_ready = sem("t2_ready")
        as_hi = sem("as_hi")
        as_ready = sem("as_ready")
        y2_full = sem("y2_full")
        out_ready = sem("out_ready")
        out_stored = sem("out_stored")

        block = es.enter_context(nc.Block())

        def first_use(it):
            return it * BODY + (MAIN0 + QUARTERS)

        def head_cols(j):
            return slice(j * HEADS4 * TOK, (j + 1) * HEADS4 * TOK)

        def each_step(eng, body):
            for g in range(G):
                with eng.Fori(0, B - 1) as b:
                    body(b + g * B, g, b, NEXT_BATCH)
                body(g * B + B - 1, g, B - 1, NEXT_GROUP if g == 0 else LAST)

        @block.sync
        def _(sp):
            def load(slot, width, src, rows=128):
                sp.dma_start(stage[0:rows, slot, 0:width], src).then_inc(staged[slot], 16)

            def load_x():
                for t in range(NT):
                    sp.dma_start(x_t[:, t, :], x[t * TT:(t + 1) * TT, :]).then_inc(x_loaded[t], 16)

            def load_next(n, width, src, rows=128):
                sp.wait_ge(split_done, n - 1)
                load(n % 2, width, src, rows)

            def parts(l0, dl, turn_batch):
                for q in range(QUARTERS):
                    sp.wait_ge(split_done, dl + (l0 + q - 1))
                    load((l0 + q) % 2, NF * PW[q], part(turn_batch, q))

            load_x()
            load(0, W4, wq[4])
            load(1, W4, wq[5])
            sp.dma_start(gates[:, 0:1], gx.partition_broadcast(128)).then_inc(small_loaded, 16)
            sp.dma_start(gates[:, 1:2], gf.partition_broadcast(128)).then_inc(small_loaded, 16)
            sp.dma_start(a13_raw[:, :, :], a13).then_inc(small_loaded, 16)
            spilled = 0
            for n, what in enumerate(FIRST):
                if n < 2:
                    continue
                if what[0] == "q":
                    load_next(n, W4, wq[(int(what[1]) + 4) % NG4])
                elif what[0] == "c":
                    q = int(what[1])
                    load_next(n, NF * PW[q], part(ctx[0], q))
                else:
                    load_next(n, W4, wk[0] if what == "k" else wv[0])
                if n >= L_WK and spilled < 4 and what[0] != "q":
                    sp.wait_ge(use_done, LN_USES + HEADS4 * (spilled + 1))
                    sp.dma_start(q_dram[:, head_cols(spilled)],
                                 qo[:, head_cols(spilled)]).then_inc(q_spilled[spilled], 16)
                    spilled += 1
            for g in range(G):
                with sp.Fori(0, B - 1) as b:
                    parts(L_LOOP[g], b * QUARTERS, ctx[b + 1])
                if g > 0:
                    break
                load_next(L_SWITCH, W4, wk[1])
                load_next(L_SWITCH + 1, NF * PW[0], part(ctx[0], 0))

                def exchange(j):
                    sp.wait_ge(use_done, first_use(B - 1) + U_O[j] + 1)
                    sp.dma_start(o_dram[:, head_cols(j)], qo[:, head_cols(j)]).then_inc(o_spilled[j], 16)
                    sp.wait_ge(q_spilled[j], 16)
                    sp.wait_ge(o_spilled[j], 16)
                    sp.dma_start(qo[:, head_cols(j)], q_dram[:, head_cols(j)]).then_inc(q_loaded[j], 16)

                exchange(0)
                exchange(1)
                for q in range(1, QUARTERS):
                    load_next(L_SWITCH + 1 + q, NF * PW[q], part(ctx[0], q))
                load_next(L_SWITCH + 5, W4, wv[1])
                exchange(2)
                exchange(3)

            for k in range(NG4):
                load_next(L_WO + k, W4, wo[(k + 4) % NG4])
                if 2 <= k < 6:
                    sp.wait_ge(ot_ready, k - 1)
                    sp.dma_start(qo[:, head_cols(k - 2)], o_dram[:, head_cols(k - 2)]).then_inc(o_loaded[k - 2], 16)
            load_x()
            load_next(L_FFN, HID, w1)
            load_next(L_FFN + 1, HID, w3)
            load_next(L_FFN + 2, HID, b13[:, 0, :], 4)
            load_next(L_FFN + 3, HID, b13[:, 1, :], 4)
            load_next(L_FFN + 4, 2 * len(HCH), a2)
            load_next(L_FFN + 5, F, b2, 2)
            load_next(L_FFN + 6, 3 * F, w2)
            for t in range(NT):
                sp.wait_ge(out_ready, t + 1)
                sp.dma_start(out[t * TT:(t + 1) * TT, :], x_t[:, t, :]).then_inc(out_stored, 16)
            sp.wait_ge(out_stored, NT * 16)
            sp.wait_ge(small_loaded, 3 * 16)

        @block.gpsimd
        def _(pool):
            nc.gpsimd.memset(ident[:, :], 0.0).then_inc(ident_zeroed, 1)
            pool.wait_ge(ident_zeroed, 1)
            nc.gpsimd.affine_select(out=ident[:, :], in_=ident[:, :], compare_op=ALU.not_equal, fill=1.0,
                                    base=0, pattern=[[-1, 128]], channel_multiplier=1).then_inc(ident_ready, 1)

            def lo_part(n, slot, width, hi, lo, rows=128):
                pool.wait_ge(split_hi, n + 1)
                nc.gpsimd.tensor_tensor(lo, stage[0:rows, slot, 0:width], hi.bitcast(F32),
                                        ALU.subtract).then_inc(split_done, 1)

            def ctx_lo(n, slot, q):
                lo_part(n, slot, NF * PW[q], part(cx_hi, q), part(cx_lo, q))

            for n, what in enumerate(FIRST):
                if what[0] == "q" and (n == 0 or n >= L_WQ[4]):
                    continue
                if n == 1 or n > L_WQ[4]:
                    pool.wait_ge(split_done, n)
                if what[0] == "q":
                    lo_part(n, n % 2, W4, wq_hi[int(what[1]) % 2], wq_lo[int(what[1]) % 2])
                elif what[0] == "c":
                    ctx_lo(n, n % 2, int(what[1]))
                elif what == "k":
                    lo_part(n, n % 2, W4, wk_hi[:, :], wk_lo[:, :])
                else:
                    lo_part(n, n % 2, W4, wv_hi[:, :], wv_lo[:, :])

            def body(it, g, b, then):
                if then == NEXT_BATCH:
                    for q in range(QUARTERS):
                        ctx_lo(b * QUARTERS + (L_LOOP[g] + q), q % 2, q)
                elif then == NEXT_GROUP:
                    lo_part(L_SWITCH, 0, W4, wk_hi[:, :], wk_lo[:, :])
                    for q in range(QUARTERS):
                        ctx_lo(L_SWITCH + 1 + q, (1 + q) % 2, q)
                    lo_part(L_SWITCH + 5, 1, W4, wv_hi[:, :], wv_lo[:, :])

            each_step(pool, body)
            for k in range(NG4):
                lo_part(L_WO + k, k % 2, W4, wo_hi[k % 2], wo_lo[k % 2])
            lo_part(L_FFN, 0, HID, w1h, w1l)
            lo_part(L_FFN + 1, 1, HID, w3h, w3l)
            lo_part(L_FFN + 2, 0, HID, b1h, b1l, 4)
            lo_part(L_FFN + 3, 1, HID, b3h, b3l, 4)
            lo_part(L_FFN + 4, 0, 2 * len(HCH), a2h, a2l)
            lo_part(L_FFN + 5, 1, F, b2h, b2l, 2)
            lo_part(L_FFN + 6, 0, 3 * F, wk_hi[:, 0:3 * F], wk_lo[:, 0:3 * F])
            for c, (_, n, j) in enumerate(HCH):
                pool.wait_ge(act_ready, c + 1)
                ac = act_t[c % 2][0:n, :]
                if c < 3:
                    nc.gpsimd.tensor_copy(asum[0:n, j, :], ac).then_inc(act_summed, 1)
                else:
                    pool.wait_ge(act_summed, c - 2)
                    nc.gpsimd.tensor_tensor(asum[0:n, j, :], asum[0:n, j, :], ac, ALU.add).then_inc(act_summed, 1)

        @block.scalar
        def _(act):
            copy = ACT.Copy

            def hi_part(l0, width, hi, later=0, rows=128):
                slot = l0 % 2
                act.wait_ge(staged[slot], later * 16 + (l0 // 2 + 1) * 16)
                nc.scalar.activation(hi, stage[0:rows, slot, 0:width], copy).then_inc(split_hi, 1)

            def take(n, dst, src):
                act.wait_ge(use_full, n + 1)
                nc.scalar.activation(dst, src, copy).then_inc(use_hi, 1)

            def layernorm_std(i):
                for t in range(NT):
                    act.wait_ge(var_ready, i * NT + t + 1)
                    nc.scalar.activation(std[0:TT, t:t + 1], std[0:TT, t:t + 1], ACT.Sqrt).then_inc(std_ready, 1)

            layernorm_std(0)
            hi_part(L_WQ[0], W4, wq_hi[0])
            for f in range(NF):
                take(f, xT[:, 0, f, :], banks[:, LN_BANKS[f], 0:TOK])
            hi_part(L_WQ[1], W4, wq_hi[1])
            for k in range(NG4):
                for j in range(HEADS4):
                    if j == 2:
                        if k == 2:
                            hi_part(L_WK, W4, wk_hi[:, :])
                        elif k > 2 and k < 3 + QUARTERS:
                            hi_part(L_CTX0[k - 3], NF * PW[k - 3], part(cx_hi, k - 3))
                    n = LN_USES + k * HEADS4 + j
                    if k >= 4 and j == 0:
                        act.wait_ge(q_spilled[k - 4], 16)
                    h = (k % 4) * HEADS4 + j
                    act.wait_ge(use_full, n + 1)
                    nc.scalar.activation(qo[:, h * TOK:(h + 1) * TOK], ring[n % 2][:, 0:TOK], copy,
                                         scale=SCALE).then_inc(use_done, 1)
                if k + 2 < NG4:
                    hi_part(L_WQ[k + 2], W4, wq_hi[k % 2])
            hi_part(L_WV, W4, wv_hi[:, :])

            def k_use(n, bank, q):
                take(n, k_hi[:, P0[q]:P0[q] + PW[q]], ring[bank][:, 0:PW[q]])

            def v_use(n, c):
                take(n, vh[0:CH, c, :], banks[0:CH, V_BANKS[c % 4], 0:VW])

            def o_use(n, bank):
                take(n, otmp[:, :], ring[bank][:, 2 * ROWS:4 * ROWS])

            def exp_half(step, h):
                act.wait_ge(max_ready, step * 2 + h + 1)
                nc.scalar.activation(ph[0:ROWS, h, :].rearrange("p (t n) -> p t n", t=THIRDS),
                                     banks[0:ROWS, 3 * h:3 * h + 3, 0:T3], ACT.Exp, bias=negmax[0:ROWS, h:h + 1],
                                     accum_out=row_sum[0:ROWS, h:h + 1]).then_inc(exp_ready, 1)

            def transposed(step):
                for h, j in TR:
                    act.wait_ge(tr_full, step * len(TR) + (h * NPT + j + 1))
                    nc.scalar.activation(
                        pt6[0:CH, j, :, 0, h, :],
                        banks[0:CH, 3 * h + j, 0:CPB * ROWS].rearrange("p (c r) -> p c r", c=CPB),
                        copy).then_inc(tr_hi, 1)

            def split_q(it, g, b, p):
                if g == 1:
                    act.wait_ge(q_loaded[p], 16)
                h = slice(p * REP, (p + 1) * REP)
                nc.scalar.activation(qsh3[:, h, :], qo3[:, h, bass.ts(b, TQ)], copy).then_inc(qs_hi_ready, 1)

            def split_out(k):
                nc.scalar.activation(ot_hi[k % 2], qo[:, head_cols(k % 4)], copy).then_inc(ot_hi_ready, 1)

            def body(it, g, b, then):
                u = first_use(it)
                step = it * PAIRS
                split_q(it, g, b, 0)
                for c in range(V_USES):
                    v_use(u + c, c)
                for p in range(PAIRS):
                    exp_half(step + p, 0)
                    if p == 3:
                        exp_half(step + p, 1)
                        o_use(u + U_O[2], U_O[2] % 2)
                        if then == LAST:
                            transposed(step + p)
                            split_out(0)
                            o_use(u + U_O[3] - QUARTERS, U_O[3] % 2)
                            return
                    k0 = U_K0 if p == 3 else U_K[p + 1]
                    if p == 3:
                        if then == NEXT_BATCH:
                            hi_part(L_LOOP[g] + 3, NF * PW[3], part(cx_hi, 3), later=b * 2)
                        else:
                            hi_part(L_SWITCH + 4, NF * PW[3], part(cx_hi, 3))
                    k_use(u + k0, k0 % 2, 0)
                    if then == NEXT_GROUP and p == 3:
                        hi_part(L_SWITCH + 5, W4, wv_hi[:, :])
                    if p < 3:
                        exp_half(step + p, 1)
                    k_use(u + k0 + 1, (k0 + 1) % 2, 1)
                    k_use(u + k0 + 2, k0 % 2, 2)
                    if p < 3:
                        split_q(it, g, b, p + 1)
                    transposed(step + p)
                    k_use(u + k0 + 3, (k0 + 1) % 2, 3)
                    if p != 2:
                        o_use(u + U_O[p], U_O[p] % 2)
                        continue
                    if then == NEXT_GROUP:
                        hi_part(L_SWITCH, W4, wk_hi[:, :])
                    for q in range(QUARTERS):
                        for c in range(PC0[q], PC0[q] + PCH[q]):
                            v_use(u + U_V23 + c, c)
                        if q == 3 and then != LAST:
                            continue
                        if then == NEXT_BATCH:
                            hi_part(L_LOOP[g] + q, NF * PW[q], part(cx_hi, q), later=b * 2)
                        elif then == NEXT_GROUP:
                            hi_part(L_SWITCH + 1 + q, NF * PW[q], part(cx_hi, q))
                        elif q in (1, 3):
                            hi_part(L_WO + q // 2, W4, wo_hi[q // 2])

            for q in range(QUARTERS):
                k_use(MAIN0 + q, q % 2, q)
            each_step(act, body)

            act.wait_ge(small_loaded, 3 * 16)
            nc.scalar.activation(tgate[:, :], gates[:, :], ACT.Tanh).then_inc(gate_ready, 1)
            nc.scalar.activation(a13_hi[:, :, :], a13_raw[:, :, :], copy).then_inc(a_hi, 1)
            for k in range(1, NG4):
                if k >= 2:
                    act.wait_ge(blk_used, k - 1)
                    hi_part(L_WO + k, W4, wo_hi[k % 2])
                if k == 3:
                    act.wait_ge(use_done, END)
                if k >= 4:
                    act.wait_ge(o_loaded[k - 4], 16)
                split_out(k)
            hi_part(L_FFN, HID, w1h)
            hi_part(L_FFN + 1, HID, w3h)
            hi_part(L_FFN + 2, HID, b1h, rows=4)
            layernorm_std(1)
            hi_part(L_FFN + 3, HID, b3h, rows=4)
            hi_part(L_FFN + 4, 2 * len(HCH), a2h)
            act.wait_ge(y_full, NT)
            for i, f in enumerate(LN2_ORDER):
                take(END + i, xT[:, 0, f, :], banks[:, LN_BANKS[f], 0:TOK])
            hi_part(L_FFN + 5, F, b2h, rows=2)
            act.wait_ge(t13_full, 1)
            nc.scalar.activation(t13h, banks[0:4, T13_BANK, 0:TOK], copy, scale=LORA).then_inc(t13_hi, 1)
            hi_part(L_FFN + 6, 3 * F, wk_hi[:, 0:3 * F])

            def split_act(c):
                n = HCH[c][1]
                act.wait_ge(act_ready, c + 1)
                if c >= 2:
                    act.wait_ge(down_done, c - 1)
                nc.scalar.activation(acth[c % 2][0:n, :], act_t[c % 2][0:n, :], copy).then_inc(act_hi, 1)

            def sum_hi(j):
                n = HCUT[j][1]
                act.wait_ge(act_summed, len(HCH) - 3 + j + 1)
                nc.scalar.activation(ash[0:n, j, :], asum[0:n, j, :], copy).then_inc(as_hi, 1)

            for c, (_, n, _) in enumerate(HCH):
                if c >= 1:
                    split_act(c - 1)
                if c == len(HCH) - 1:
                    sum_hi(0)
                act.wait_ge(h_full, c + 1)
                if c >= 2:
                    act.wait_ge(act_ready, c - 1)
                nc.scalar.activation(th_t[c % 2][0:n, :], banks[0:n, H_BANKS[c % 3][0], 0:TOK], ACT.Tanh,
                                     scale=0.5).then_inc(h_tanh, 1)
            split_act(len(HCH) - 1)
            sum_hi(1)
            sum_hi(2)
            act.wait_ge(down_done, len(HCH))
            nc.scalar.activation(t2h, banks[0:2, T2_BANK, 0:TOK], copy, scale=LORA).then_inc(t2_hi, 1)

        @block.vector
        def _(dve):
            def rest(n, dst, src, hi, skipped=Q_USES):
                dve.wait_ge(use_hi, n + 1 - skipped)
                nc.vector.tensor_tensor(dst, src, hi.bitcast(F32), ALU.subtract).then_inc(use_done, 1)

            def variance(i, t):
                s = 2 * t + max(t - 1, 0) if i == 0 else NT * 3 + t * 4
                nc.vector.bn_stats(stats[0:TT, t, :], x_t[:, t, :]).then_inc(ln_step, 1)
                dve.wait_ge(ln_step, s + 1)
                nc.vector.bn_aggr(mv[0:TT, t, :], stats[0:TT, t, :]).then_inc(ln_step, 1)
                dve.wait_ge(ln_step, s + 2)
                nc.vector.tensor_scalar(std[0:TT, t:t + 1], mv[0:TT, t, 1:2], EPS, None,
                                        ALU.add).then_inc(var_ready, 1)

            def row_sums(t):
                dve.wait_ge(ln_step, NT * 3 + t * 4 + 4)
                nc.vector.tensor_reduce(xn_t[:, t, F:F + 128], xn_t[:, t, 0:F].rearrange("p (f n) -> p n f", f=NF),
                                        AX.X, ALU.add).then_inc(xn_ready, 1)

            def normalise_rows(i, t):
                s = min(3 * t + 2, 3 * NT - 3) if i == 0 else NT * 3 + t * 4
                dve.wait_ge(std_ready, i * NT + t + 1)
                nc.vector.reciprocal(rstd[0:TT, t:t + 1], std[0:TT, t:t + 1]).then_inc(ln_step, 1)
                dve.wait_ge(ln_step, s + 3)
                ins = nc.vector.tensor_scalar(xn_t[:, t, 0:F], x_t[:, t, :], mv[0:TT, t, 0:1], rstd[0:TT, t:t + 1],
                                              ALU.subtract, ALU.mult)
                ins.then_inc(xn_ready if i == 0 else ln_step, 1)

            for t in range(NT):
                dve.wait_ge(x_loaded[t], 16)
                variance(0, t)
                if t >= 1:
                    normalise_rows(0, t - 1)
            normalise_rows(0, NT - 1)
            for f in range(NF):
                rest(f, xT[:, 1, f, :], banks[:, LN_BANKS[f], 0:TOK], xT[:, 0, f, :], skipped=0)
            for k in (0, *range(4, NG4)):
                n = L_WQ[k]
                dve.wait_ge(split_hi, n + 1)
                if n > 0:
                    dve.wait_ge(split_done, n)
                nc.vector.tensor_tensor(wq_lo[k % 2], stage[:, n % 2, 0:W4], wq_hi[k % 2].bitcast(F32),
                                        ALU.subtract).then_inc(split_done, 1)

            def k_use(n, bank, q):
                c = slice(P0[q], P0[q] + PW[q])
                rest(n, k_lo[:, c], ring[bank][:, 0:PW[q]], k_hi[:, c])

            def v_use(n, c):
                rest(n, vl[0:CH, c, :], banks[0:CH, V_BANKS[c % 4], 0:VW], vh[0:CH, c, :])

            def o_use(n, bank, b, p, skipped=Q_USES):
                dve.wait_ge(use_hi, n + 1 - skipped)
                nc.vector.tensor_tensor(qo3[:, p * REP:(p + 1) * REP, bass.ts(b, TQ)],
                                        ring[bank][:, 0:2 * ROWS].rearrange("p (h t) -> p h t", h=REP),
                                        otmp[:, :].rearrange("p (h t) -> p h t", h=REP),
                                        ALU.add).then_inc(use_done, 1)

            def max_half(step, h):
                dve.wait_ge(score_full, step * 2 + h + 1)
                nc.vector.tensor_reduce(negmax[0:ROWS, h:h + 1], banks[0:ROWS, 3 * h:3 * h + 3, 0:T3], AX.XY,
                                        ALU.max, negate=True).then_inc(max_ready, 1)

            def normalise(step, h):
                n = step * 2 + h + 1
                dve.wait_ge(exp_ready, n)
                nc.vector.reciprocal(rinv[0:ROWS, h:h + 1], row_sum[0:ROWS, h:h + 1]).then_inc(recip_ready, 1)
                dve.wait_ge(recip_ready, n)
                nc.vector.tensor_scalar(ph[0:ROWS, h, :], ph[0:ROWS, h, :], rinv[0:ROWS, h:h + 1], None,
                                        ALU.mult).then_inc(prob_ready, 1)

            def transposed(step):
                for h, j in TR:
                    dve.wait_ge(tr_hi, step * len(TR) + (h * NPT + j + 1))
                    nc.vector.tensor_tensor(
                        pt6[0:CH, j, :, 1, h, :],
                        banks[0:CH, 3 * h + j, 0:CPB * ROWS].rearrange("p (c r) -> p c r", c=CPB),
                        pt6[0:CH, j, :, 0, h, :].bitcast(F32), ALU.subtract).then_inc(tr_done, 1)

            def split_q(it, b, p):
                dve.wait_ge(qs_hi_ready, it * PAIRS + (p + 1))
                h = slice(p * REP, (p + 1) * REP)
                nc.vector.tensor_tensor(qsl3[:, h, :], qo3[:, h, bass.ts(b, TQ)], qsh3[:, h, :].bitcast(F32),
                                        ALU.subtract).then_inc(qs_ready, 1)

            def split_out(k):
                dve.wait_ge(ot_hi_ready, k + 1)
                nc.vector.tensor_tensor(ot_lo[k % 2], qo[:, head_cols(k % 4)], ot_hi[k % 2].bitcast(F32),
                                        ALU.subtract).then_inc(ot_ready, 1)

            def body(it, g, b, then):
                u = first_use(it)
                step = it * PAIRS
                split_q(it, b, 0)
                for c in range(V_USES):
                    v_use(u + c, c)
                for p in range(PAIRS):
                    max_half(step + p, 0)
                    max_half(step + p, 1)
                    normalise(step + p, 0)
                    if p == 3:
                        o_use(u + U_O[2], U_O[2] % 2, b, 2)
                        normalise(step + p, 1)
                        if then == LAST:
                            transposed(step + p)
                            split_out(0)
                            o_use(u + U_O[3] - QUARTERS, U_O[3] % 2, b, 3)
                            return
                    k0 = U_K0 if p == 3 else U_K[p + 1]
                    k_use(u + k0, k0 % 2, 0)
                    if p < 3:
                        normalise(step + p, 1)
                    k_use(u + k0 + 1, (k0 + 1) % 2, 1)
                    k_use(u + k0 + 2, k0 % 2, 2)
                    if p < 3:
                        split_q(it, b, p + 1)
                    transposed(step + p)
                    k_use(u + k0 + 3, (k0 + 1) % 2, 3)
                    if p != 2:
                        o_use(u + U_O[p], U_O[p] % 2, b, p)
                        continue
                    for c in range(V_USES):
                        v_use(u + U_V23 + c, c)

            for q in range(QUARTERS):
                k_use(MAIN0 + q, q % 2, q)
            each_step(dve, body)

            dve.wait_ge(a_hi, 1)
            nc.vector.tensor_tensor(a13_lo[:, :, :], a13_raw[:, :, :], a13_hi[:, :, :].bitcast(F32),
                                    ALU.subtract).then_inc(a_ready, 1)
            for k in range(1, NG4):
                split_out(k)
            dve.wait_ge(gate_ready, 1)
            for t in range(NT):
                dve.wait_ge(x_loaded[t], 2 * 16)
                dve.wait_ge(y_full, t + 1)
                nc.vector.scalar_tensor_tensor(x_t[:, t, :], banks[0:TT, t, :], tgate[0:TT, 0:1], x_t[:, t, :],
                                               ALU.mult, ALU.add).then_inc(x1_ready, 1)
                dve.wait_ge(x1_ready, t + 1)
                variance(1, t)
                if t >= 1:
                    row_sums(t - 1)
                normalise_rows(1, t)
            row_sums(NT - 1)
            for i, f in enumerate(LN2_ORDER):
                rest(END + i, xT[:, 1, f, :], banks[:, LN_BANKS[f], 0:TOK], xT[:, 0, f, :])
            dve.wait_ge(t13_hi, 1)
            nc.vector.scalar_tensor_tensor(t13l, banks[0:4, T13_BANK, 0:TOK], LORA, t13h.bitcast(F32),
                                           ALU.mult, ALU.subtract).then_inc(t13_ready, 1)

            def split_act(c):
                n = HCH[c][1]
                dve.wait_ge(act_hi, c + 1)
                nc.vector.tensor_tensor(actl[c % 2][0:n, :], act_t[c % 2][0:n, :],
                                        acth[c % 2][0:n, :].bitcast(F32), ALU.subtract).then_inc(act_split, 1)

            def sum_lo(j):
                n = HCUT[j][1]
                dve.wait_ge(as_hi, j + 1)
                nc.vector.tensor_tensor(asl[0:n, j, :], asum[0:n, j, :], ash[0:n, j, :].bitcast(F32),
                                        ALU.subtract).then_inc(as_ready, 1)

            for c, (_, n, _) in enumerate(HCH):
                th = th_t[c % 2][0:n, :]
                gate, up = (banks[0:n, bank, 0:TOK] for bank in H_BANKS[c % 3])
                if c >= 1:
                    split_act(c - 1)
                if c == len(HCH) - 1:
                    sum_lo(0)
                dve.wait_ge(h_tanh, c + 1)
                nc.vector.scalar_tensor_tensor(th, th, 1.0, gate, ALU.add, ALU.mult).then_inc(ffn_step, 1)
                dve.wait_ge(ffn_step, c + 1)
                if c >= 2:
                    dve.wait_ge(act_summed, c - 1)
                    dve.wait_ge(act_split, c - 1)
                nc.vector.scalar_tensor_tensor(act_t[c % 2][0:n, :], up, 0.5, th,
                                               ALU.mult, ALU.mult).then_inc(act_ready, 1)
            split_act(len(HCH) - 1)
            sum_lo(1)
            sum_lo(2)
            dve.wait_ge(t2_hi, 1)
            nc.vector.scalar_tensor_tensor(t2l, banks[0:2, T2_BANK, 0:TOK], LORA, t2h.bitcast(F32),
                                           ALU.mult, ALU.subtract).then_inc(t2_ready, 1)
            for t in range(NT):
                dve.wait_ge(y2_full, t + 1)
                nc.vector.scalar_tensor_tensor(x_t[:, t, :], banks[0:TT, t, :], tgate[0:TT, 1:2], x_t[:, t, :],
                                               ALU.mult, ALU.add).then_inc(out_ready, 1)

        @block.tensor
        def _(pe):
            def three(dst, ah, al, bh, bl, first, last):
                nc.tensor.matmul(dst, ah, bh, start=first, stop=False)
                nc.tensor.matmul(dst, ah, bl, start=False, stop=False)
                return nc.tensor.matmul(dst, al, bh, start=False, stop=last)

            def bank_free(n):
                pe.wait_ge(use_done, n - 1)

            def transposes(t, order):
                for f in order:
                    ins = nc.tensor.transpose(banks[:, LN_BANKS[f], t * TT:(t + 1) * TT],
                                              xn_t[:, t, f * 128:(f + 1) * 128], ident[0:TT, 0:TT])
                    if t == NT - 1:
                        ins.then_inc(use_full, 1)

            pe.wait_ge(ident_ready, 1)
            for t in range(NT):
                pe.wait_ge(xn_ready, t + 1)
                transposes(t, range(NF))
            pe.wait_ge(use_done, LN_USES)
            for k in range(NG4):
                pe.wait_ge(split_done, L_WQ[k] + 1)
                wh, wl = w4(wq_hi[k % 2]), w4(wq_lo[k % 2])
                for j in range(HEADS4):
                    n = LN_USES + k * HEADS4 + j
                    bank_free(n)
                    for f in range(NF):
                        ins = three(ring[n % 2][:, 0:TOK], wh[:, f, j * D:(j + 1) * D], wl[:, f, j * D:(j + 1) * D],
                                    xT[:, 0, f, :], xT[:, 1, f, :], f == 0, f == NF - 1)
                    ins.then_inc(use_full, 1)

            def k_use(n, bank, p, q, values=None):
                if values is not None:
                    pe.wait_ge(use_done, values)
                else:
                    bank_free(n)
                c = slice(p * D, (p + 1) * D)
                for f in range(NF):
                    ins = three(ring[bank][:, 0:PW[q]], wkh[:, f, c], wkl[:, f, c], cxh[q][:, f, :], cxl[q][:, f, :],
                                f == 0, f == NF - 1)
                ins.then_inc(use_full, 1)

            def v_use(n, s, c):
                if c == 0:
                    bank_free(n)
                elif c == 2:
                    pe.wait_ge(use_done, n - 2)
                elif c >= 4:
                    pe.wait_ge(use_done, n - 3)
                q = max(i for i in range(QUARTERS) if PC0[i] <= c)
                i = slice((c - PC0[q]) * CH, (c - PC0[q] + 1) * CH)
                dst = banks[0:CH, V_BANKS[c % 4], 0:VW]
                for f in range(NF):
                    ins = three(dst, cxh[q][:, f, i], cxl[q][:, f, i], wvh[:, f, s * VW:(s + 1) * VW],
                                wvl[:, f, s * VW:(s + 1) * VW], f == 0, f == NF - 1)
                ins.then_inc(use_full, 1)

            def scores(step, p, keys_done, banks_done):
                pe.wait_ge(use_done, keys_done)
                pe.wait_ge(qs_ready, step + 1)
                for h in range(2):
                    if h == 1 and banks_done is not None:
                        pe.wait_ge(use_done, banks_done)
                    r = slice((p * REP + 2 * h) * TQ, (p * REP + 2 * h) * TQ + ROWS)
                    for t in range(THIRDS):
                        c = slice(t * T3, (t + 1) * T3)
                        ins = three(banks[0:ROWS, 3 * h + t, 0:T3], qs_hi[:, r], qs_lo[:, r], k_hi[:, c], k_lo[:, c],
                                    True, True)
                    ins.then_inc(score_full, 1)

            def transpose_probs(step):
                for h, j in TR:
                    if j == 0:
                        pe.wait_ge(prob_ready, step * 2 + h + 1)
                    for c in range(CPB):
                        at = (j * CPB + c) * CH
                        ins = nc.tensor.transpose(banks[0:CH, 3 * h + j, c * ROWS:(c + 1) * ROWS],
                                                  ph[0:ROWS, h, at:at + CH], ident[0:ROWS, 0:ROWS])
                    ins.then_inc(tr_full, 1)

            def weigh(n, bank, step, p):
                bank_free(n)
                i = slice(p % 2 * D, (p % 2 + 1) * D)
                dst, hi_rows = ring[bank][:, 0:4 * ROWS], ring[bank][:, 0:2 * ROWS]
                for c in range(NCH):
                    if c % CPB == 0:
                        pe.wait_ge(tr_done, step * len(TR) + (NPT + c // CPB + 1))
                    if c > 0:
                        nc.tensor.matmul(hi_rows, vl[0:CH, c, i], pt3[0:CH, c, 0:2 * ROWS], start=False, stop=False)
                    ins = nc.tensor.matmul(dst, vh[0:CH, c, i], pt3[0:CH, c, :], start=(c == 0), stop=(c == NCH - 1))
                    if c == 0:
                        nc.tensor.matmul(hi_rows, vl[0:CH, c, i], pt3[0:CH, c, 0:2 * ROWS], start=False, stop=False)
                ins.then_inc(use_full, 1)

            def body(it, g, b, then):
                u = first_use(it)
                step = it * PAIRS
                for c in range(V_USES):
                    v_use(u + c, 0, c)
                for p in range(3):
                    k0 = U_K[p + 1]
                    if p == 0:
                        scores(step, 0, u - 1, u + V_USES)
                    else:
                        scores(step + p, p, u + U_O[p - 1], None)
                    for q in range(3):
                        k_use(u + k0 + q, (k0 + q) % 2, p + 1, q,
                              values=u + V_USES - 3 + 2 * q if p == 0 and q < 2 else None)
                    transpose_probs(step + p)
                    k_use(u + k0 + 3, (k0 + 3) % 2, p + 1, 3)
                    if p < 2:
                        weigh(u + U_O[p], U_O[p] % 2, step + p, p)
                pe.wait_ge(tr_done, step * len(TR) + 3 * len(TR))
                for c in range(V_USES):
                    v_use(u + U_V23 + c, 1, c)
                scores(step + 3, 3, u + U_V23, u + U_O[2])
                pe.wait_ge(use_done, u + U_O[2])
                weigh(u + U_O[2], U_O[2] % 2, step + 2, 2)
                if then == LAST:
                    transpose_probs(step + 3)
                    weigh(u + U_O[3] - QUARTERS, U_O[3] % 2, step + 3, 3)
                    return
                for q in range(QUARTERS):
                    if q == 3:
                        transpose_probs(step + 3)
                    if then == NEXT_BATCH:
                        pe.wait_ge(split_done, b * QUARTERS + (L_LOOP[g] + q + 1))
                    else:
                        pe.wait_ge(split_done, L_SWITCH + 1 + q + 1)
                    k_use(u + U_K0 + q, (U_K0 + q) % 2, 0, q)
                if then == NEXT_GROUP:
                    pe.wait_ge(split_done, L_SWITCH + 5 + 1)
                weigh(u + U_O[3], U_O[3] % 2, step + 3, 3)

            for q in range(QUARTERS):
                pe.wait_ge(split_done, L_CTX0[q] + 1)
                k_use(MAIN0 + q, q % 2, 0, q)
            pe.wait_ge(split_done, L_WV + 1)
            each_step(pe, body)

            pe.wait_ge(tr_done, G * B * PAIRS * len(TR))
            def project(k, j, t):
                c = slice(j * TOK + t * TT, j * TOK + (t + 1) * TT)
                wh, wl = w4(wo_hi[k % 2]), w4(wo_lo[k % 2])
                return three(banks[0:TT, t, :], ot_hi[k % 2][:, c], ot_lo[k % 2][:, c], wh[:, j, :], wl[:, j, :],
                             k == 0 and j == 0, k == NG4 - 1 and j == HEADS4 - 1)

            for k in range(NG4 - 1):
                pe.wait_ge(split_done, L_WO + k + 1)
                pe.wait_ge(ot_ready, k + 1)
                for j in range(HEADS4):
                    for t in range(NT):
                        ins = project(k, j, t)
                ins.then_inc(blk_used, 1)

            def turn(t):
                pe.wait_ge(xn_ready, NT + t + 1)
                transposes(t, LN2_ORDER)

            pe.wait_ge(split_done, L_WO + NG4)
            pe.wait_ge(ot_ready, NG4)
            for t in range(NT):
                for j in range(HEADS4):
                    ins = project(NG4 - 1, j, t)
                ins.then_inc(y_full, 1)
                if t == 2:
                    turn(0)
            for t in range(1, NT):
                turn(t)

            def hidden(c):
                at, n, _ = HCH[c]
                hid = slice(at, at + n)
                for bank, wh, wl in zip(H_BANKS[c % 3], (w1h, w3h), (w1l, w3l)):
                    three(banks[0:n, bank, 0:TOK], wh[:, hid], wl[:, hid], xT[:, 0, NF, :], xT[:, 1, NF, :],
                          True, False)

            def lora_up(c):
                at, n, _ = HCH[c]
                hid = slice(at, at + n)
                for bank, bh, bl in zip(H_BANKS[c % 3], (b1h, b3h), (b1l, b3l)):
                    ins = three(banks[0:n, bank, 0:TOK], bh[:, hid], bl[:, hid], t13h, t13l, False, True)
                ins.then_inc(h_full, 1)

            pe.wait_ge(split_done, L_FFN + 2)
            pe.wait_ge(use_done, END + 1)
            hidden(0)
            pe.wait_ge(a_ready, 1)
            for f in range(NF):
                pe.wait_ge(use_done, END + 2 + f)
                ins = three(banks[0:4, T13_BANK, 0:TOK], a13_hi[:, f, :], a13_lo[:, f, :],
                            xT[:, 0, f, :], xT[:, 1, f, :], f == 0, f == NF - 1)
            ins.then_inc(t13_full, 1)

            def lora_down(c):
                n = HCH[c][1]
                a = slice(2 * c, 2 * c + 2)
                pe.wait_ge(act_split, c + 1)
                three(banks[0:2, T2_BANK, 0:TOK], a2h[0:n, a], a2l[0:n, a], acth[c % 2][0:n, :], actl[c % 2][0:n, :],
                      c == 0, c == len(HCH) - 1).then_inc(down_done, 1)

            for c in range(1, len(HCH)):
                if c >= 3:
                    pe.wait_ge(act_ready, c - 2)
                hidden(c)
                if c >= 3:
                    lora_down(c - 3)
                if c == 1:
                    pe.wait_ge(split_done, L_FFN + 5)
                    pe.wait_ge(t13_ready, 1)
                lora_up(c - 1)
            lora_up(len(HCH) - 1)
            lora_down(len(HCH) - 3)
            def down(j):
                n = HCUT[j][1]
                pe.wait_ge(as_ready, j + 1)
                for t in range(NT):
                    c = slice(t * TT, (t + 1) * TT)
                    three(banks[0:TT, t, :], ash[0:n, j, c], asl[0:n, j, c], w2h[0:n, j, :], w2l[0:n, j, :],
                          j == 0, False)

            pe.wait_ge(split_done, L_FFN + 7)
            pe.wait_ge(act_ready, len(HCH) - 1)
            down(0)
            lora_down(len(HCH) - 2)
            down(1)
            lora_down(len(HCH) - 1)
            down(2)
            pe.wait_ge(t2_ready, 1)
            for t in range(NT):
                c = slice(t * TT, (t + 1) * TT)
                three(banks[0:TT, t, :], t2h[:, c], t2l[:, c], b2h, b2l, False, True).then_inc(y2_full, 1)


def kernel(x, ctx_4096, g_xattn, g_ffn, L0_xattn_wq, L0_xattn_wk, L0_xattn_wv, L0_xattn_wo, L0_ffn_w1q,
           L0_ffn_a1, L0_ffn_b1, L0_ffn_w3q, L0_ffn_a3, L0_ffn_b3, L0_ffn_w2q, L0_ffn_a2, L0_ffn_b2):
    import numpy as np
    import concourse.bacc as bacc
    from concourse.bass_utils import run_bass_kernel_spmd as run

    c = np.ascontiguousarray

    def blocks(w, n):
        w = np.asarray(w)
        return c(w.reshape(NF, 128, n, -1).transpose(2, 1, 0, 3).reshape(n, 128, -1))

    ctx = np.asarray(ctx_4096).reshape(B, TK, NF, 128).transpose(0, 3, 2, 1)
    ctx = np.concatenate([ctx[..., P0[q]:P0[q] + PW[q]].reshape(B, 128, -1) for q in range(QUARTERS)], -1)
    w2t = np.zeros((3 * 128, F), np.float32)
    w2t[:HQR] = np.asarray(L0_ffn_w2q).T
    a2t = np.zeros((128, len(HCH), 2), np.float32)
    for i, (at, n, _) in enumerate(HCH):
        a2t[:n, i] = np.asarray(L0_ffn_a2)[:, at:at + n].T
    b13 = np.zeros((4, 2, HID), np.float32)
    b13[0:2, 0], b13[2:4, 1] = np.asarray(L0_ffn_b1).T, np.asarray(L0_ffn_b3).T
    a13 = np.concatenate([np.asarray(L0_ffn_a1), np.asarray(L0_ffn_a3)], 0)
    arrays = {
        "x": c(np.asarray(x).reshape(TOK, F)),
        "ctx": c(ctx),
        "gx": c(np.asarray(g_xattn)[:1]),
        "gf": c(np.asarray(g_ffn)[:1]),
        "wq": blocks(L0_xattn_wq, NG4),
        "wk": blocks(L0_xattn_wk, G),
        "wv": blocks(L0_xattn_wv, G),
        "wo": c(np.asarray(L0_xattn_wo).reshape(NG4, HEADS4, D, F).transpose(0, 2, 1, 3).reshape(NG4, 128, -1)),
        "w1": c(np.asarray(L0_ffn_w1q).T),
        "w3": c(np.asarray(L0_ffn_w3q).T),
        "w2": c(w2t.reshape(3, 128, F).transpose(1, 0, 2).reshape(128, 3 * F)),
        "a13": c(a13.T.reshape(NF, 128, 4).transpose(1, 0, 2)),
        "a2": a2t.reshape(128, -1),
        "b13": b13,
        "b2": c(np.asarray(L0_ffn_b2).T),
    }
    nc = bacc.Bacc("TRN2", target_bir_lowering=False, num_devices=1)
    args = [nc.dram_tensor(n, a.shape, mybir.dt.from_np(a.dtype), kind="ExternalInput").ap() for n, a in arrays.items()]
    out = nc.dram_tensor("out", (TOK, F), F32, kind="ExternalOutput").ap()
    q_dram = nc.dram_tensor("q_dram", (128, GH * TOK), F32).ap()
    o_dram = nc.dram_tensor("o_dram", (128, GH * TOK), F32).ap()
    flamingo_kernel(nc, *args, out, q_dram, o_dram)
    r = run(nc, [arrays], core_ids=[0])
    return r.results[0]["out"].reshape(B, TQ, F)
```
